# Optimizing a Trainium2 kernel written in Bass

```python
import numpy as np
import jax
import jax.numpy as jnp

def _softmax(x, axis=-1):
    return jax.nn.softmax(x, axis=axis)

def _gelu(x):
    return jax.nn.gelu(x, approximate=True)

def _silu(x):
    return jax.nn.silu(x)

def _sigmoid(x):
    return jax.nn.sigmoid(x)

def _layernorm(x, axis=-1, eps=1e-05):
    m = jnp.mean(x, axis=axis, keepdims=True)
    v = jnp.var(x, axis=axis, keepdims=True)
    return (x - m) / jnp.sqrt(v + eps)

def _scatter_add(tgt, idx, src, axis=0):
    return tgt.at[idx].add(src)

def _segment_sum(src, seg, n):
    return jax.ops.segment_sum(src, seg, n)
kernel_name = 'mk_macaron_d1_jaxref_r8_869317'

def setup_inputs(seed: int=0):
    np.random.seed(seed)
    _w = jnp.asarray

    def _L0_attn_setup():
        import math
        import jax, jax.numpy as jnp
        import numpy as np
        B, L, HID = (2, 256, 256)
        H = 16
        D = HID // H
        EPS = 1e-06
        ROPE_BASE = 10000.0
        BETA_MIN, BETA_MAX = (0.8, 0.9995)

        def _rope_cache(seq_len, dim):
            half = dim // 2
            inv_freq = 1.0 / ROPE_BASE ** (jnp.arange(half, dtype=jnp.float32) / float(half))
            t = jnp.arange(seq_len, dtype=jnp.float32)
            freqs = t[:, None] * inv_freq[None, :]
            return (jnp.cos(freqs), jnp.sin(freqs))

        def _apply_rope(x, cos, sin):
            half = x.shape[-1] // 2
            xe, xo = (x[..., :half], x[..., half:])
            c = cos[None, None]
            s = sin[None, None]
            return jnp.concatenate([xe * c - xo * s, xe * s + xo * c], axis=-1)

        def _deltanet(x, Wq, Wk, Wv, Wg, bg, Wo, bo):
            Bb, Ll, _ = x.shape
            split = lambda t: t.reshape(Bb, Ll, H, D).transpose(0, 2, 1, 3)
            q = split(x @ Wq)
            k = split(x @ Wk)
            v = split(x @ Wv)
            cos, sin = _rope_cache(Ll, D)
            q = _apply_rope(q, cos, sin)
            k = _apply_rope(k, cos, sin)
            beta = jax.nn.sigmoid(x @ Wg + bg)
            beta = jnp.clip(beta, BETA_MIN, BETA_MAX).transpose(0, 2, 1)
            phi_q = jax.nn.elu(q) + 1.0
            phi_k = jax.nn.elu(k) + 1.0
            pq = phi_q.transpose(2, 0, 1, 3)
            pk = phi_k.transpose(2, 0, 1, 3)
            vt = v.transpose(2, 0, 1, 3)
            bt = beta.transpose(2, 0, 1)
            S0 = jnp.zeros((Bb, H, D, D), jnp.float32)
            z0 = jnp.zeros((Bb, H, D), jnp.float32)

            def step(carry, inp):
                S, z = carry
                pq_t, pk_t, v_t, b_t = inp
                S = S * b_t[..., None, None] + pk_t[..., :, None] * v_t[..., None, :]
                z = z * b_t[..., None] + pk_t
                numer = jnp.einsum('bhd,bhde->bhe', pq_t, S)
                denom = jnp.sum(pq_t * z, axis=-1, keepdims=True) + EPS
                return ((S, z), numer / denom)
            (_, _), y = jax.lax.scan(step, (S0, z0), (pq, pk, vt, bt))
            y = y.transpose(1, 0, 2, 3).reshape(Bb, Ll, HID)
            return y @ Wo + bo
        key = jax.random.key(seed)
        ks = jax.random.split(key, 6)
        sc = 1.0 / math.sqrt(HID)
        return {'x': jax.random.normal(ks[0], (B, L, HID), jnp.float32), 'Wq': jax.random.normal(ks[1], (HID, HID), jnp.float32) * sc, 'Wk': jax.random.normal(ks[2], (HID, HID), jnp.float32) * sc, 'Wv': jax.random.normal(ks[3], (HID, HID), jnp.float32) * sc, 'Wg': jax.random.normal(ks[4], (HID, H), jnp.float32) * sc, 'bg': jnp.full((H,), math.log(0.98 / (1.0 - 0.98)), jnp.float32), 'Wo': jax.random.normal(ks[5], (HID, HID), jnp.float32) * sc, 'bo': jnp.zeros((HID,), jnp.float32)}
    _L0_attn_in = _L0_attn_setup()

    def _L0_ffn_setup():
        import jax, jax.numpy as jnp
        import numpy as np
        B, L, D = (2, 128, 256)
        E, K = (8, 2)
        H, HS = (176, 352)
        key = jax.random.key(seed)
        ks = jax.random.split(key, 9)
        s = 0.02
        return {'x': jax.random.normal(ks[0], (B, L, D), dtype=jnp.float32), 'gate_w': jax.random.normal(ks[1], (E, D), dtype=jnp.float32) * s, 'w_gate': jax.random.normal(ks[2], (E, D, H), dtype=jnp.float32) * s, 'w_up': jax.random.normal(ks[3], (E, D, H), dtype=jnp.float32) * s, 'w_down': jax.random.normal(ks[4], (E, H, D), dtype=jnp.float32) * s, 'shgate_w': jax.random.normal(ks[5], (D,), dtype=jnp.float32) * s, 'shw_gate': jax.random.normal(ks[6], (D, HS), dtype=jnp.float32) * s, 'shw_up': jax.random.normal(ks[7], (D, HS), dtype=jnp.float32) * s, 'shw_down': jax.random.normal(ks[8], (HS, D), dtype=jnp.float32) * s}
    _L0_ffn_in = _L0_ffn_setup()
    _d = {'L0_attn_x': _L0_attn_in['x'], 'L0_attn_Wq': _L0_attn_in['Wq'], 'L0_attn_Wk': _L0_attn_in['Wk'], 'L0_attn_Wv': _L0_attn_in['Wv'], 'L0_attn_Wg': _L0_attn_in['Wg'], 'L0_attn_bg': _L0_attn_in['bg'], 'L0_attn_Wo': _L0_attn_in['Wo'], 'L0_attn_bo': _L0_attn_in['bo'], 'L0_ffn_gate_w': _L0_ffn_in['gate_w'], 'L0_ffn_w_gate': _L0_ffn_in['w_gate'], 'L0_ffn_w_up': _L0_ffn_in['w_up'], 'L0_ffn_w_down': _L0_ffn_in['w_down'], 'L0_ffn_shgate_w': _L0_ffn_in['shgate_w'], 'L0_ffn_shw_gate': _L0_ffn_in['shw_gate'], 'L0_ffn_shw_up': _L0_ffn_in['shw_up'], 'L0_ffn_shw_down': _L0_ffn_in['shw_down']}
    _x0 = _d['L0_attn_x']
    _d['L0_attn_x'] = jax.random.normal(jax.random.fold_in(jax.random.key(seed), 1), (4, 1024, 256), dtype=_x0.dtype)
    del _x0
    return _d

def reference(L0_attn_x, L0_attn_Wq, L0_attn_Wk, L0_attn_Wv, L0_attn_Wg, L0_attn_bg, L0_attn_Wo, L0_attn_bo, L0_ffn_gate_w, L0_ffn_w_gate, L0_ffn_w_up, L0_ffn_w_down, L0_ffn_shgate_w, L0_ffn_shw_gate, L0_ffn_shw_up, L0_ffn_shw_down):

    def _L0_attn_ref(x, Wq, Wk, Wv, Wg, bg, Wo, bo):
        import math
        import jax, jax.numpy as jnp
        import numpy as np
        B, L, HID = (2, 256, 256)
        H = 16
        D = HID // H
        EPS = 1e-06
        ROPE_BASE = 10000.0
        BETA_MIN, BETA_MAX = (0.8, 0.9995)

        def _rope_cache(seq_len, dim):
            half = dim // 2
            inv_freq = 1.0 / ROPE_BASE ** (jnp.arange(half, dtype=jnp.float32) / float(half))
            t = jnp.arange(seq_len, dtype=jnp.float32)
            freqs = t[:, None] * inv_freq[None, :]
            return (jnp.cos(freqs), jnp.sin(freqs))

        def _apply_rope(x, cos, sin):
            half = x.shape[-1] // 2
            xe, xo = (x[..., :half], x[..., half:])
            c = cos[None, None]
            s = sin[None, None]
            return jnp.concatenate([xe * c - xo * s, xe * s + xo * c], axis=-1)

        def _deltanet(x, Wq, Wk, Wv, Wg, bg, Wo, bo):
            Bb, Ll, _ = x.shape
            split = lambda t: t.reshape(Bb, Ll, H, D).transpose(0, 2, 1, 3)
            q = split(x @ Wq)
            k = split(x @ Wk)
            v = split(x @ Wv)
            cos, sin = _rope_cache(Ll, D)
            q = _apply_rope(q, cos, sin)
            k = _apply_rope(k, cos, sin)
            beta = jax.nn.sigmoid(x @ Wg + bg)
            beta = jnp.clip(beta, BETA_MIN, BETA_MAX).transpose(0, 2, 1)
            phi_q = jax.nn.elu(q) + 1.0
            phi_k = jax.nn.elu(k) + 1.0
            pq = phi_q.transpose(2, 0, 1, 3)
            pk = phi_k.transpose(2, 0, 1, 3)
            vt = v.transpose(2, 0, 1, 3)
            bt = beta.transpose(2, 0, 1)
            S0 = jnp.zeros((Bb, H, D, D), jnp.float32)
            z0 = jnp.zeros((Bb, H, D), jnp.float32)

            def step(carry, inp):
                S, z = carry
                pq_t, pk_t, v_t, b_t = inp
                S = S * b_t[..., None, None] + pk_t[..., :, None] * v_t[..., None, :]
                z = z * b_t[..., None] + pk_t
                numer = jnp.einsum('bhd,bhde->bhe', pq_t, S)
                denom = jnp.sum(pq_t * z, axis=-1, keepdims=True) + EPS
                return ((S, z), numer / denom)
            (_, _), y = jax.lax.scan(step, (S0, z0), (pq, pk, vt, bt))
            y = y.transpose(1, 0, 2, 3).reshape(Bb, Ll, HID)
            return y @ Wo + bo
        return _deltanet(x, Wq, Wk, Wv, Wg, bg, Wo, bo)

    def _L0_ffn_ref(x, gate_w, w_gate, w_up, w_down, shgate_w, shw_gate, shw_up, shw_down):
        import jax, jax.numpy as jnp
        import numpy as np
        B, L, D = (2, 128, 256)
        E, K = (8, 2)
        H, HS = (176, 352)
        b, l, d = x.shape
        xf = x.reshape(-1, d)
        logits = jnp.einsum('td,ed->te', xf.astype(jnp.float32), gate_w)
        probs = jax.nn.softmax(logits.astype(jnp.float32), axis=-1)
        weights, indices = jax.lax.top_k(probs, K)
        weights = (weights / weights.sum(-1, keepdims=True)).astype(x.dtype)
        onehot = jax.nn.one_hot(indices, E, dtype=x.dtype)
        combine = jnp.einsum('tk,tke->te', weights, onehot)
        g = jnp.einsum('td,edh->teh', xf, w_gate)
        u = jnp.einsum('td,edh->teh', xf, w_up)
        h = jax.nn.silu(g) * u
        out = jnp.einsum('teh,ehd,te->td', h.astype(jnp.float32), w_down.astype(jnp.float32), combine.astype(jnp.float32))
        sgate = jax.nn.sigmoid(xf @ shgate_w)[:, None]
        sh = jax.nn.silu(xf @ shw_gate) * (xf @ shw_up) @ shw_down
        out = out + (sgate * sh).astype(jnp.float32)
        return out.astype(x.dtype).reshape(b, l, d)
    x = L0_attn_x
    x = x + 0.5 * _L0_ffn_ref(_layernorm(x, axis=-1), L0_ffn_gate_w, L0_ffn_w_gate, L0_ffn_w_up, L0_ffn_w_down, L0_ffn_shgate_w, L0_ffn_shw_gate, L0_ffn_shw_up, L0_ffn_shw_down)
    x = x + _L0_attn_ref(_layernorm(x, axis=-1), L0_attn_Wq, L0_attn_Wk, L0_attn_Wv, L0_attn_Wg, L0_attn_bg, L0_attn_Wo, L0_attn_bo)
    x = x + 0.5 * _L0_ffn_ref(_layernorm(x, axis=-1), L0_ffn_gate_w, L0_ffn_w_gate, L0_ffn_w_up, L0_ffn_w_down, L0_ffn_shgate_w, L0_ffn_shw_gate, L0_ffn_shw_up, L0_ffn_shw_down)
    return x

_drawn_inputs = setup_inputs


def setup_inputs(seed=0):
    import zlib

    import numpy as np

    out = dict(_drawn_inputs(seed))
    spreads = {'L0_attn_bg': (3.891820192337036, 0.2), 'L0_attn_bo': (0.0, 0.1)}
    factors = {'L0_attn_Wq': 3.128,
     'L0_attn_Wg': 2.952,
     'L0_ffn_gate_w': 6.897,
     'L0_ffn_w_gate': 6.031,
     'L0_ffn_w_up': 5.977,
     'L0_ffn_w_down': 5.959,
     'L0_ffn_shgate_w': 8.0,
     'L0_ffn_shw_gate': 5.836,
     'L0_ffn_shw_up': 5.763,
     'L0_ffn_shw_down': 5.757}
    for name, (base, spread) in spreads.items():
        noise = np.random.default_rng([zlib.crc32(name.encode()), seed]).standard_normal(out[name].shape)
        drawn = base * np.exp(spread * noise) if base else spread * noise
        out[name] = jnp.asarray(drawn.astype(out[name].dtype))
    for name, factor in factors.items():
        out[name] = (out[name] * factor).astype(out[name].dtype)
    return out
```

```python
import concourse.bass as bass
from concourse import mybir
from collections import namedtuple
from contextlib import ExitStack
import numpy as np

F32 = mybir.dt.float32
F32R = mybir.dt.float32r
U32 = mybir.dt.uint32
ALU = mybir.AluOpType
ACT = mybir.ActivationFunctionType
AX = mybir.AxisListType

B, L, D = 4, 1024, 256
HEADS, DH = 16, 16
E, HE, HS = 8, 176, 352
P = 128
KD = D // P
GT = 4
GN = GT * P
NT = B * L // P
NG = NT // GT
XR = 4
STAGE = 7 * D
HID = E * HE + HS
FT = -(-HID // P)
HE_ALL = E * HE
NR = E + 2
VW = DH + 2
QKV = 3 * D + HEADS
LN_EPS, DEN_EPS = 1e-5, 1e-6
BETA_MIN, BETA_MAX = 0.8, 0.9995

C_ID = 0
C_CAUSAL = C_ID + P
C_BLOCK = C_CAUSAL + P
C_ROPE = C_BLOCK + 8 * VW
C_PAR = C_ROPE + NT * 16
C_IOTA = C_PAR + 2
C_KEEP = C_IOTA + E
C_EXP = C_KEEP + NT
C_HALF = C_EXP + 2 * P
C_ALL = C_HALF + GT


def constants():
    c = np.zeros((P, C_ALL), np.float32)
    p = np.arange(P)
    c[:, C_ID:C_ID + P] = np.eye(P)
    c[:, C_CAUSAL:C_CAUSAL + P] = p[:, None] <= p[None, :]
    c[:, C_BLOCK:C_BLOCK + 8 * VW] = (p[:, None] // DH) == (np.arange(8 * VW)[None, :] // VW)
    half = DH // 2
    inv = (np.float32(1.0) / np.float32(10000.0) ** (np.arange(half, dtype=np.float32) / np.float32(half))).astype(np.float32)
    ang = (np.arange(L, dtype=np.float32)[:, None] * inv[None, :]).astype(np.float32)
    tab = np.concatenate([np.cos(ang), np.sin(ang)], 1).astype(np.float32)
    tab = tab.reshape(L // P, P, 16).transpose(1, 0, 2)
    c[:, C_ROPE:C_ROPE + NT * 16] = np.tile(tab, (1, B, 1)).reshape(P, NT * 16)
    c[:, C_PAR] = (p // DH) % 2 == 0
    c[:, C_PAR + 1] = (p // DH) % 2 == 1
    c[:, C_IOTA:C_IOTA + E] = np.arange(E)
    c[:, C_KEEP:C_KEEP + NT] = (np.arange(NT) % (L // P)) != L // P - 1
    for h in range(HEADS):
        c[h, C_EXP + h * DH:C_EXP + (h + 1) * DH] = 1.0
    c[:, C_HALF:C_HALF + GT] = -0.5
    return c


def selector():
    c = np.zeros((2 * NR, HID), np.float32)
    for r in (0, NR):
        for e in range(E + 1):
            c[r + e, e * HE:(e + 1) * HE if e < E else HID] = 1.0
    return c


Group = namedtuple("Group", "at x")


def group(g):
    return Group(g, g % XR * GT)


def need(eng, sem, value):
    if not isinstance(value, int) or value > 0:
        eng.wait_ge(sem, value)


def bc(ap, axis, n):
    v = ap.unsqueeze(axis)
    s = list(v.shape)
    s[axis] = n
    return v.broadcast_to(s)


U_CHUNK = 10
U_NORM = 4
U_LOOP = GT * U_CHUNK + 3 * U_NORM
U_HEAD = 3 * U_NORM


def attention_slots(g, hb, k0):
    out = {}
    k = k0
    for c in range(GT):
        for stage, slot, uses in (("proj", 0, 2), ("turn", 1, 1), ("core", 2, 5)):
            if stage == "proj" and c > 0:
                out.setdefault(3 * c, []).append(("wo", g, c - 1, hb, k))
                k += 2
            out.setdefault(3 * c + slot, []).append((stage, g, c, hb, k))
            k += uses
    out.setdefault(3 * GT, []).append(("wo", g, GT - 1, hb, k))
    return out


def head():
    yield ("norm", "F1", 0, group(0), 0, 0, None, 0)
    for j in range(FT):
        yield ("ffn", "F1", 0, j)
    yield ("tail_a", 0)
    yield ("tail_b", 0, group(0), False)
    yield ("norm", "F1", 1, group(1), 0, U_NORM, 0, 1)
    yield ("norm", "A", 2, group(0), 0, 2 * U_NORM, None, None)


def body(i, last, before, this, after):
    hb = (i - 1) * (U_LOOP // 2) + U_HEAD // 2
    a = attention_slots(before, hb, 0)
    ku = GT * U_CHUNK
    n1, n2 = 2 * i - 1, 2 * i
    for j in range(FT):
        yield ("ffn", "F1", n1, j)
        yield from a.get(j, ())
    yield ("norm", "F2", 3 * i, before, hb, ku, 2 * i - 2, n2)
    ku += U_NORM
    for j in range(FT):
        yield ("ffn", "F2", n2, j)
        if j == 0:
            yield ("tail_a", n1)
        if j == 1:
            yield ("tail_b", n1, this, False)
        if j == 3 and not last:
            yield ("norm", "F1", 3 * i + 1, after, hb, ku, n1, n2 + 1)
            ku += U_NORM
        if j == 8:
            yield ("norm", "A", 3 * i + 2 - last, this, hb, ku, i, None)
            ku += U_NORM
    yield ("tail_a", n2)
    yield ("tail_b", n2, before, True)


def end():
    i, g = NG, group(NG - 1)
    hb = (i - 1) * (U_LOOP // 2) + U_HEAD // 2 - U_NORM // 2
    a = attention_slots(g, hb, 0)
    for j in range(3 * GT + 1):
        yield from a[j]
    yield ("norm", "F2", 3 * i - 1, g, hb, GT * U_CHUNK, 2 * i - 2, 2 * i - 1)
    for j in range(FT):
        yield ("ffn", "F2", 2 * i - 1, j)
    yield ("tail_a", 2 * i - 1)
    yield ("tail_b", 2 * i - 1, g, True)


def run(eng, do):
    for s in head():
        do(*s)
    with eng.Fori(1, NG - 1) as i:
        gs = [Group(i + k, eng.snap((i + k) % XR * GT)) for k in (-1, 0, 1)]
        for s in body(i, 0, *gs):
            do(*s)
    for s in body(NG - 1, 1, group(NG - 2), group(NG - 1), None):
        do(*s)
    for s in end():
        do(*s)


def build(nc, x_d, wq_d, wk_d, wv_d, wg_d, bg_d, wo_d, bo_d, gw_d, eg_d, eu_d, ed_d, sgw_d, sg_d, su_d, sd_d, c_d, sel_d, out_d):
    ctx = ExitStack()
    with ctx:
        def sb(name, shape, dt=F32):
            return ctx.enter_context(nc.sbuf_tensor(name, shape, dt))

        def pb(name):
            return ctx.enter_context(nc.psum_tensor(name, [P, 512], F32))

        def sem(name):
            return ctx.enter_context(nc.semaphore(name))

        X = sb("X", [P, XR * GT, D])
        CN = sb("CN", [P, C_ALL])
        SEL = sb("SEL", [2 * NR, HID], F32R)
        WG = [sb(f"WG{k}", [P, KD, HID], F32R) for k in "hl"]
        WU = [sb(f"WU{k}", [P, KD, HID], F32R) for k in "hl"]
        WD = [sb(f"WD{k}", [P, FT, D], F32R) for k in "hl"]
        WP = [sb(f"WP{k}", [P, KD, QKV], F32R) for k in "hl"]
        WO = [sb(f"WO{k}", [P, KD, D], F32R) for k in "hl"]
        R32 = sb("R32", [P, KD, NR])
        WR = [sb(f"WR{k}", [P, KD, NR], F32R) for k in "hl"]
        BO = sb("BO", [P, D])
        HBG = sb("HBG", [HEADS, 1])
        ST = sb("ST", [P, GT, 6])
        MV = sb("MV", [P, GT, 2])
        VE = sb("VE", [P, GT])
        RS = sb("RS", [P, GT])
        XT = {k: [sb(f"XT{k}{h}", [P, KD, GN], F32R) for h in "hl"] for k in ("F1", "A", "F2")}
        LG = sb("LG", [P, GT, NR])
        TOP = sb("TOP", [P, GT, 8])
        IDX = sb("IDX", [P, GT, 8], U32)
        IDF = sb("IDF", [P, GT, 2])
        GAP = sb("GAP", [P, GT])
        E2 = sb("E2", [P, GT])
        SGT = sb("SGT", [P, GT])
        DEN2 = sb("DEN2", [P, GT])
        W12 = sb("W12", [P, 2, GT])
        HOT = sb("HOT", [P, 2, GT, E])
        CMB = sb("CMB", [P, GT, NR])
        CHL = sb("CHL", [P, GT, 2 * NR])
        CT = {k: sb(f"CT{k}", [2 * NR, GN], F32R) for k in ("F1", "F2")}
        CBS = [sb(f"CBS{k}", [P, GN]) for k in range(2)]
        TH = [sb(f"TH{k}", [P, GN]) for k in range(2)]
        HH = [sb(f"HH{k}", [P, GN], F32R) for k in range(2)]
        HL = [sb(f"HL{k}", [P, GN], F32R) for k in range(2)]
        BT = sb("BT", [HEADS, GN])
        ZR = sb("ZR", [HEADS, P])
        DP = sb("DP", [HEADS, GN])
        DEC = sb("DEC", [P, GT, 2 * HEADS])
        PT = sb("PT", [P, 2, GT])
        SCRATCH = sb("SCRATCH", [P, 2 * STAGE])
        STG = [SCRATCH[:, k * STAGE:(k + 1) * STAGE] for k in range(2)]
        RC, RT, QK0, QK1 = (SCRATCH[:, k * 2 * D:(k + 1) * 2 * D] for k in range(4))
        QK = [QK0, QK1]
        XN = SCRATCH[:, 8 * D:12 * D].rearrange("p (t d) -> p t d", t=GT)
        AM1 = SCRATCH[:, 12 * D:14 * D].rearrange("p (h t) -> p h t", h=4)
        VA = [sb(f"VA{k}", [P, HEADS, VW]) for k in range(2)]
        QT = sb("QT", [P, 2, P])
        KT = [sb(f"KT{k}", [P, 2, P]) for k in range(2)]
        AM = [sb("AM0", [P, 4, P]), AM1]
        S = sb("S", [P, 2, 8 * VW])
        DS = sb("DS", [P, 2, 8 * VW])
        DN = sb("DN", [P, HEADS])
        RD = sb("RD", [P, HEADS])
        Y = sb("Y", [P, HEADS, DH])
        YT = [sb(f"YT{k}", [P, KD, P], F32R) for k in "hl"]

        T = [pb(f"T{k}") for k in range(2)]
        T2 = pb("T2")
        PG, PU, PC = pb("PG"), pb("PU"), pb("PC")
        PY = [pb(f"PY{k}") for k in range(2)]

        ident = CN[:, C_ID:C_ID + P]
        rope = CN[:, C_ROPE:C_ROPE + NT * 16].rearrange("p (t c) -> p t c", c=16)
        expand = CN[0:HEADS, C_EXP:C_EXP + 2 * P].rearrange("p (a c) -> p a c", a=2)
        block2 = bc(CN[:, C_BLOCK:C_BLOCK + 8 * VW], 1, 2)

        s_const, s_x0, s_x1, s_xrest, s_small, s_bo = (sem(n) for n in (
            "const_loaded", "x0_loaded", "x1_loaded", "xrest_loaded", "router_loaded", "bo_loaded"))
        s_stage = [sem(f"stage{k}_loaded") for k in range(2)]
        s_hi, s_lo, s_prep, s_wready = sem("weight_high"), sem("weight_low"), sem("prepared"), sem("weights_ready")
        s_tr = [sem(f"tmp{k}_ready") for k in range(2)]
        s_tf = [sem(f"tmp{k}_free") for k in range(2)]
        s_var, s_rstd, s_xn, s_xh = sem("var"), sem("rstd"), sem("xn"), sem("xt_high")
        s_gap, s_e2, s_comb, s_ct = sem("gap"), sem("top2_exp"), sem("comb"), sem("comb_turned")
        s_cb, s_cbs, s_g, s_th, s_u, s_w, s_s = (sem(n) for n in (
            "comb_spread", "comb_copied", "gate", "gate_tanh", "up", "up_weighted", "gate_silu"))
        s_h, s_hh, s_hl, s_down, s_yr = (sem(n) for n in (
            "hidden", "hidden_high", "hidden_low", "down", "y_added"))
        s_dp, s_dec, s_boa = sem("decay"), sem("decay_turned"), sem("bo_added")
        s_rt, s_ro, s_mn, s_ex, s_qk = (sem(n) for n in (
            "rope_parts", "rope_sum", "phi_min", "phi_exp", "qk_scaled"))
        s_inter, s_or, s_st = (sem(n) for n in ("inter", "core_read", "state"))
        s_av, s_yhi, s_out, s_store = sem("scores_used"), sem("attn_y_high"), sem("out_ready"), sem("stored")

        xt_view = x_d.rearrange("b (t p) d -> p (b t) d", p=P)
        ot_view = out_d.rearrange("b (t p) d -> p (b t) d", p=P)
        block = ctx.enter_context(nc.Block())

        def kcols(w, k):
            return w[k * P:(k + 1) * P, :]

        def expert_piece(w, s, dst, k):
            return ([((P, 0, HE_ALL, E), w[:, k * P:(k + 1) * P, :].rearrange("e p h -> p e h")),
                     ((P, HE_ALL, HID, 0), kcols(s, k))],
                    [(P, 0, HID, dst[0][:, k, :], dst[1][:, k, :])])

        split = FT // 2
        fe, fs = HE_ALL // P, (HID - HE_ALL) // P
        rest = HID - (fe + fs) * P
        pieces = [expert_piece(eg_d, sg_d, WG, 0), expert_piece(eg_d, sg_d, WG, 1),
                  expert_piece(eu_d, su_d, WU, 0), expert_piece(eu_d, su_d, WU, 1)]
        edf = ed_d.rearrange("e h d -> (e h) d")
        pieces.append(([((P, 0, split * D, split), edf[0:split * P, :].rearrange("(t p) d -> p t d", p=P))],
                       [(P, 0, split * D, WD[0][:, 0:split, :], WD[1][:, 0:split, :])]))
        n2 = fe - split
        pieces.append((
            [((P, 0, n2 * D, n2), edf[split * P:HE_ALL, :].rearrange("(t p) d -> p t d", p=P)),
             ((P, n2 * D, (n2 + fs) * D, fs), sd_d[0:fs * P, :].rearrange("(t p) d -> p t d", p=P)),
             ((rest, (n2 + fs) * D, (n2 + fs + 1) * D, 0), sd_d[fs * P:HS, :])],
            [(P, 0, (n2 + fs) * D, WD[0][:, split:FT - 1, :], WD[1][:, split:FT - 1, :]),
             (rest, (n2 + fs) * D, (n2 + fs + 1) * D, WD[0][0:rest, FT - 1, :], WD[1][0:rest, FT - 1, :])]))
        loads = [((P, k * QKV + w * D, k * QKV + w * D + m.shape[1], 0), kcols(m, k))
                 for w, m in enumerate((wq_d, wk_d, wv_d, wg_d)) for k in range(KD)]
        pieces.append((loads, [(P, 0, KD * QKV, WP[0][:, :, :], WP[1][:, :, :])]))
        pieces.append(([((P, 0, KD * D, KD), wo_d.rearrange("(k p) n -> p k n", p=P))],
                       [(P, 0, KD * D, WO[0][:, :, :], WO[1][:, :, :])]))
        pieces.insert(0, ([((2 * NR, 0, HID, 0), sel_d)], [(2 * NR, 0, HID, SEL[:, :], None)]))
        staged = [0, 0]
        arrive = []
        for k, (ld, _) in enumerate(pieces):
            staged[k % 2] += 16 * len(ld)
            arrive.append(staged[k % 2])
        splits = [len(c) for _, c in pieces]

        def shaped(ap, like):
            if len(like.shape) == 2:
                return ap
            return ap.rearrange("p (a b) -> p a b", a=like.shape[1])

        @block.sync
        def _(sp):
            sp.dma_start(X[:, 0:GT, :], xt_view[:, 0:GT, :]).then_inc(s_x0, 16)
            sp.dma_start(CN[:, :], c_d).then_inc(s_const, 16)
            for k, (ld, _) in enumerate(pieces):
                if k >= 2:
                    sp.wait_ge(s_lo, sum(splits[:k - 1]))
                for (rows, a, b, t), src in ld:
                    dst = STG[k % 2][0:rows, a:b]
                    if t:
                        dst = dst.rearrange("p (t n) -> p t n", t=t)
                    sp.dma_start(dst, src).then_inc(s_stage[k % 2], 16)
                if k == 3:
                    sp.dma_start(X[:, GT:2 * GT, :], xt_view[:, GT:2 * GT, :]).then_inc(s_x1, 16)
            sp.dma_start(BO[:, :], bo_d.rearrange("(a n) -> a n", a=1).broadcast_to([P, D])).then_inc(s_bo, 16)
            sp.dma_start(X[:, 2 * GT:3 * GT, :], xt_view[:, 2 * GT:3 * GT, :]).then_inc(s_xrest, 16)
            sp.wait_ge(s_xrest, 16)
            sp.dma_start(X[:, 3 * GT:4 * GT, :], xt_view[:, 3 * GT:4 * GT, :]).then_inc(s_xrest, 16)
            for g in range(NG):
                at = g % XR * GT
                sp.wait_ge(s_out, g + 1)
                sp.dma_start(ot_view[:, g * GT:(g + 1) * GT, :], X[:, at:at + GT, :]).then_inc(s_store, 16)
                if g + XR < NG:
                    sp.wait_ge(s_store, 16 * g + 16)
                    sp.wait_ge(s_xrest, 16 * g + 32)
                    sp.dma_start(X[:, at:at + GT, :], xt_view[:, (g + XR) * GT:(g + XR + 1) * GT, :]).then_inc(s_xrest, 16)
            sp.wait_ge(s_store, 16 * NG)

        @block.gpsimd
        def _(pool):
            pool.wait_ge(s_prep, 1)
            with nc.allow_non_contiguous_dma("router columns"):
                for k in range(KD):
                    pool.dma_start(R32[:, k, 0:E], gw_d[:, k * P:(k + 1) * P].rearrange("e p -> p e")).then_inc(s_small, 16)
                    pool.dma_start(R32[:, k, E:E + 1], sgw_d[k * P:(k + 1) * P].rearrange("(p a) -> p a", a=1)).then_inc(s_small, 16)
                pool.dma_start(HBG[:, :], bg_d.rearrange("(p a) -> p a", a=1)).then_inc(s_small, 16)
            for k in range(2):
                nc.gpsimd.memset(VA[k][:, :, :], 1.0)
            nc.gpsimd.memset(S[:, :, :], 0.0)
            nc.gpsimd.memset(CMB[:, :, :], 0.0)
            nc.gpsimd.memset(ZR[:, :], 0.0).then_inc(s_prep, 1)
            pool.wait_ge(s_const, 16)

            def low(m, j):
                h = HID - j * P if j == FT - 1 else P
                pool.wait_ge(s_hh, m + 1)
                need(pool, s_down, m - 1)
                nc.gpsimd.tensor_tensor(HL[j % 2][0:h, :], TH[j % 2][0:h, :], HH[j % 2][0:h, :].bitcast(F32),
                                        ALU.subtract).then_inc(s_hl, 1)

            def norm(kind, r, g, hb, k0, prev, f):
                pool.wait_ge(s_var, r + 1)
                nc.gpsimd.tensor_tensor(RS[:, :], VE[:, :], CN[:, C_HALF:C_HALF + GT], ALU.pow).then_inc(s_rstd, 1)
                if kind == "A":
                    pool.wait_ge(s_xn, r + 1)
                    pool.wait_ge(s_bo, 16)
                    v = X[:, bass.ds(g.x, GT), :]
                    nc.gpsimd.tensor_tensor(v, v, bc(BO[:, :], 1, GT), ALU.add).then_inc(s_boa, 1)

            def ffn(kind, n, j):
                h = HID - j * P if j == FT - 1 else P
                m = n * FT + j
                if j > 0:
                    low(m - 1, j - 1)
                pool.wait_ge(s_s, m + 1)
                pool.wait_ge(s_w, m + 1)
                nc.gpsimd.tensor_tensor(TH[j % 2][0:h, :], TH[j % 2][0:h, :], CBS[j % 2][0:h, :], ALU.mult).then_inc(s_h, 1)

            def rope_sum(g, c, hb, k0):
                q = g.at * GT + c
                pool.wait_ge(s_rt, q + 1)
                nc.gpsimd.tensor_tensor(RC[:, :], RC[:, :], RT[:, :], ALU.add).then_inc(s_ro, 1)

            def do(step, *a):
                if step == "norm":
                    norm(*a)
                elif step == "ffn":
                    ffn(*a)
                elif step == "tail_a":
                    low(a[0] * FT + FT - 1, FT - 1)
                elif step == "proj":
                    rope_sum(*a)

            pool.sem_inc(s_ro, 1)
            run(pool, do)

        @block.scalar
        def _(act):
            act.wait_ge(s_const, 16)
            act.wait_ge(s_small, 80)
            nc.scalar.activation(WR[0][:, :, :], R32[:, :, :], ACT.Copy).then_inc(s_hi, 1)
            for k, (_, cuts) in enumerate(pieces):
                act.wait_ge(s_stage[k % 2], arrive[k])
                for rows, a, b, hi, lo in cuts:
                    nc.scalar.activation(hi, shaped(STG[k % 2][0:rows, a:b], hi), ACT.Copy).then_inc(s_hi, 1)

            def copy_high(m, j):
                h = HID - j * P if j == FT - 1 else P
                act.wait_ge(s_h, m + 1)
                need(act, s_down, m - 1)
                nc.scalar.activation(HH[j % 2][0:h, :], TH[j % 2][0:h, :], ACT.Copy).then_inc(s_hh, 1)

            def norm(kind, r, g, hb, k0, prev, f):
                for k in range(KD):
                    u = k0 + k
                    act.wait_ge(s_tr[u % 2], hb + u // 2 + 1)
                    if k == 0 and prev is not None:
                        if kind == "A":
                            need(act, s_qk, prev * GT)
                        else:
                            act.wait_ge(s_u, prev * FT + FT)
                    nc.scalar.activation(XT[kind][0][:, k, :], T[u % 2][:, :], ACT.Copy).then_inc(s_xh, 1)
                if kind == "A":
                    u = k0 + 2
                    act.wait_ge(s_tr[u % 2], hb + u // 2 + 1)
                    nc.scalar.activation(BT[:, :], T[u % 2][0:HEADS, :], ACT.Tanh, bias=HBG[:, 0:1], scale=0.5).then_inc(s_tf[u % 2], 1)
                    u = k0 + 3
                    act.wait_ge(s_tr[u % 2], hb + u // 2 + 1)
                    nc.scalar.activation(DEC[:, :, :], T[u % 2][:, 0:GT * 2 * HEADS].rearrange("p (c h) -> p c h", c=GT),
                                         ACT.Copy).then_inc(s_dec, 1)
                else:
                    act.wait_ge(s_gap, f + 1)
                    nc.scalar.activation(E2[:, :], GAP[:, :], ACT.Exp)
                    nc.scalar.activation(SGT[:, :], LG[:, :, E], ACT.Tanh, scale=0.5).then_inc(s_e2, 1)
                    u = k0 + 3
                    act.wait_ge(s_tr[u % 2], hb + u // 2 + 1)
                    nc.scalar.activation(CT[kind][:, :], T[u % 2][0:2 * NR, :], ACT.Copy).then_inc(s_tf[u % 2], 1)
                    act.wait_ge(s_tf[u % 2], hb + u // 2 + 1)
                    act.sem_inc(s_ct, 1)

            def ffn(kind, n, j):
                h = HID - j * P if j == FT - 1 else P
                m = n * FT + j
                act.wait_ge(s_cb, m + 1)
                need(act, s_h, m - 1)
                nc.scalar.activation(CBS[j % 2][0:h, :], PC[0:h, :], ACT.Copy).then_inc(s_cbs, 1)
                if j > 0:
                    copy_high(m - 1, j - 1)
                act.wait_ge(s_g, m + 1)
                need(act, s_hl, m - 1)
                nc.scalar.activation(TH[j % 2][0:h, :], PG[0:h, :], ACT.Tanh, scale=0.5).then_inc(s_th, 1)

            def proj(g, c, hb, k0):
                q = g.at * GT + c
                u = k0 + 1
                act.wait_ge(s_tr[u % 2], hb + u // 2 + 1)
                act.wait_ge(s_av, q * 4 + 4)
                nc.scalar.activation(VA[c % 2][:, :, 0:DH], T[u % 2][:, 0:D].rearrange("p (h d) -> p h d", h=HEADS),
                                     ACT.Copy).then_inc(s_tf[u % 2], 1)
                act.wait_ge(s_mn, q + 1)
                nc.scalar.activation(RT[:, :], RT[:, :], ACT.Exp).then_inc(s_ex, 1)

            def turn(g, c, hb, k0):
                q = g.at * GT + c
                act.wait_ge(s_tr[k0 % 2], hb + k0 // 2 + 1)
                act.wait_ge(s_av, q * 4 + 8)
                t = T[k0 % 2][:, :].rearrange("p (a b t) -> p a b t", a=2, b=2)
                nc.scalar.activation(QT[:, :, :], t[:, 0], ACT.Copy)
                nc.scalar.activation(KT[0][:, :, :], t[:, 1], ACT.Copy, scale=CN[:, C_PAR:C_PAR + 1])
                nc.scalar.activation(KT[1][:, :, :], t[:, 1], ACT.Copy, scale=CN[:, C_PAR + 1:C_PAR + 2]).then_inc(s_tf[k0 % 2], 1)

            def wo(g, c, hb, k0):
                q = g.at * GT + c
                act.wait_ge(s_tr[k0 % 2], hb + k0 // 2 + 1)
                nc.scalar.activation(YT[0][:, :, :], T[k0 % 2][:, 0:D].rearrange("p (k t) -> p k t", k=KD),
                                     ACT.Copy).then_inc(s_yhi, 1)

            def do(step, *a):
                if step == "norm":
                    norm(*a)
                elif step == "ffn":
                    ffn(*a)
                elif step == "tail_a":
                    copy_high(a[0] * FT + FT - 1, FT - 1)
                elif step == "proj":
                    proj(*a)
                elif step == "turn":
                    turn(*a)
                elif step == "wo":
                    wo(*a)

            run(act, do)

        @block.vector
        def _(dve):
            v = nc.vector
            v.memset(R32[:, :, :], 0.0).then_inc(s_prep, 1)
            dve.wait_ge(s_small, 80)
            v.tensor_scalar(HBG[:, :], HBG[:, :], 0.5, None, ALU.mult)
            dve.wait_ge(s_hi, 1)
            v.tensor_tensor(WR[1][:, :, :], R32[:, :, :], WR[0][:, :, :].bitcast(F32), ALU.subtract).then_inc(s_wready, 1)
            done = 1
            for k, (_, cuts) in enumerate(pieces):
                for rows, a, b, hi, lo in cuts:
                    done += 1
                    dve.wait_ge(s_hi, done)
                    if lo is None:
                        v.sem_inc(s_lo, 1)
                    else:
                        v.tensor_tensor(lo, shaped(STG[k % 2][0:rows, a:b], hi), hi.bitcast(F32), ALU.subtract).then_inc(s_lo, 1)
            dve.wait_ge(s_prep, 2)

            def settle():
                dve.drain()

            def norm(kind, r, g, hb, k0, prev, f):
                settle()
                if kind == "F1":
                    if isinstance(g.at, int) and g.at == 0:
                        dve.wait_ge(s_x0, 16)
                    elif isinstance(g.at, int) and g.at == 1:
                        dve.wait_ge(s_x1, 16)
                    else:
                        dve.wait_ge(s_xrest, 16 * g.at - 16)
                for c in range(GT):
                    v.bn_stats(ST[:, c, :], X[:, g.x + c, :])
                settle()
                for c in range(GT):
                    v.bn_aggr(MV[:, c, :], ST[:, c, :])
                settle()
                v.tensor_scalar(VE[:, :], MV[:, :, 1], LN_EPS, None, ALU.add).then_inc(s_var, 1)
                dve.wait_ge(s_rstd, r + 1)
                for c in range(GT):
                    last = v.tensor_scalar(XN[:, c, :], X[:, g.x + c, :], MV[:, c, 0:1], RS[:, c:c + 1],
                                           ALU.subtract, ALU.mult)
                last.then_inc(s_xn, 1)
                for k in range(KD):
                    u = k0 + k
                    dve.wait_ge(s_xh, r * KD + k + 1)
                    v.tensor_tensor(XT[kind][1][:, k, :], T[u % 2][:, :], XT[kind][0][:, k, :].bitcast(F32),
                                    ALU.subtract).then_inc(s_tf[u % 2], 1)
                if kind == "A":
                    decay(r, g, hb, k0)
                else:
                    router(f, hb, k0)

            def decay(r, g, hb, k0):
                dve.wait_ge(s_tf[k0 % 2], hb + (k0 + 2) // 2 + 1)
                v.tensor_scalar(BT[:, :], BT[:, :], 0.5, 0.5, ALU.mult, ALU.add)
                settle()
                v.tensor_scalar(BT[:, :], BT[:, :], BETA_MIN, BETA_MAX, ALU.max, ALU.min)
                settle()
                for c in range(GT):
                    t = slice(c * P, (c + 1) * P)
                    v.tensor_tensor_scan(DP[:, t], BT[:, t], ZR[:, :], 1.0, ALU.mult, ALU.add)
                settle()
                v.reciprocal(BT[:, :], DP[:, :]).then_inc(s_dp, 1)
                u = k0 + 3
                dve.wait_ge(s_dec, g.at + 1)
                dve.wait_ge(s_tr[u % 2], hb + u // 2 + 1)
                v.tensor_tensor(PT[:, :, :], T[u % 2][:, P:P + 2 * GT].rearrange("p (a c) -> p a c", a=2),
                                bc(CN[:, bass.ds(g.at * GT + C_KEEP, GT)], 1, 2), ALU.mult).then_inc(s_tf[u % 2], 1)

            def router(f, hb, k0):
                u = k0 + 2
                dve.wait_ge(s_tr[u % 2], hb + u // 2 + 1)
                v.tensor_copy(LG[:, :, :], T[u % 2][:, 0:GT * NR].rearrange("p (c e) -> p c e", c=GT)).then_inc(s_tf[u % 2], 1)
                settle()
                for c in range(GT):
                    v.max(TOP[:, c, :], LG[:, c, 0:E])
                settle()
                for c in range(GT):
                    v.max_index(IDX[:, c, :], TOP[:, c, :], LG[:, c, 0:E])
                v.tensor_tensor(GAP[:, :], TOP[:, :, 1], TOP[:, :, 0], ALU.subtract).then_inc(s_gap, 1)
                settle()
                v.tensor_copy(IDF[:, :, :], IDX[:, :, 0:2])
                settle()
                for k in range(2):
                    v.tensor_tensor(HOT[:, k], bc(CN[:, C_IOTA:C_IOTA + E], 1, GT), bc(IDF[:, :, k], 2, E), ALU.is_equal)
                dve.wait_ge(s_e2, f + 1)
                v.tensor_scalar(DEN2[:, :], E2[:, :], 4.0, 4.0, ALU.mult, ALU.add)
                v.tensor_scalar(CMB[:, :, E], SGT[:, :], 1.0, 0.125, ALU.add, ALU.mult)
                settle()
                v.reciprocal(W12[:, 0, :], DEN2[:, :])
                settle()
                v.tensor_tensor(W12[:, 1, :], W12[:, 0, :], E2[:, :], ALU.mult)
                settle()
                v.tensor_tensor(HOT[:, :, :, :], HOT[:, :, :, :], bc(W12[:, :, :], 3, E), ALU.mult)
                settle()
                v.tensor_tensor(CMB[:, :, 0:E], HOT[:, 0], HOT[:, 1], ALU.add)
                settle()
                v.tensor_copy(CHL[:, :, 0:NR].bitcast(F32R), CMB[:, :, :])
                settle()
                v.tensor_tensor(CHL[:, :, NR:2 * NR], CMB[:, :, :], CHL[:, :, 0:NR], ALU.subtract).then_inc(s_comb, 1)

            def ffn(kind, n, j):
                h = HID - j * P if j == FT - 1 else P
                m = n * FT + j
                dve.wait_ge(s_th, m + 1)
                v.scalar_tensor_tensor(TH[j % 2][0:h, :], TH[j % 2][0:h, :], 1.0, PG[0:h, :], ALU.add, ALU.mult).then_inc(s_s, 1)
                dve.wait_ge(s_cbs, m + 1)
                dve.wait_ge(s_u, m + 1)
                v.tensor_tensor(CBS[j % 2][0:h, :], PU[0:h, :], CBS[j % 2][0:h, :], ALU.mult).then_inc(s_w, 1)

            def tail_b(n, g, final):
                dve.wait_ge(s_down, n * FT + FT)
                for b in range(2):
                    xv = X[:, bass.ds(g.x + 2 * b, 2), :]
                    last = v.tensor_tensor(xv, PY[b][:, :].rearrange("p (t d) -> p t d", t=2), xv, ALU.add)
                    if b == 1:
                        last.then_inc(s_yr, 1)
                if final:
                    settle()
                    v.sem_inc(s_out, 1)

            def proj(g, c, hb, k0):
                q = g.at * GT + c
                u = k0
                dve.wait_ge(s_tr[u % 2], hb + u // 2 + 1)
                dve.wait_ge(s_ro, q + 1)              
                t = T[u % 2][:, :].rearrange("p (h a d) -> p h a d", a=2, d=8)
                tb = rope[:, g.at * GT + c, :]
                rc = RC[:, :].rearrange("p (h a d) -> p h a d", a=2, d=8)
                rt = RT[:, :].rearrange("p (h a d) -> p h a d", a=2, d=8)
                cos = bc(bc(tb[:, 0:8], 1, 2), 1, 2 * HEADS)
                v.tensor_tensor(rc, t, cos, ALU.mult)
                sin = bc(tb[:, 8:16], 1, 2 * HEADS)
                v.scalar_tensor_tensor(rt[:, :, 0, :], t[:, :, 1, :], -1.0, sin, ALU.mult, ALU.mult)
                v.tensor_tensor(rt[:, :, 1, :], t[:, :, 0, :], sin, ALU.mult).then_inc(s_rt, 1)
                dve.wait_ge(s_rt, q + 1)
                v.sem_inc(s_tf[u % 2], 1)
                dve.wait_ge(s_ro, q + 2)
                v.tensor_scalar(RT[:, :], RC[:, :], 0.0, None, ALU.min).then_inc(s_mn, 1)
                dve.wait_ge(s_ex, q + 1)
                v.scalar_tensor_tensor(RC[:, :], RC[:, :], 0.0, RT[:, :], ALU.max, ALU.add)
                settle()
                if c == 0:
                    dve.wait_ge(s_dec, g.at + 1)
                dve.wait_ge(s_av, q * 4 + 4)
                v.tensor_tensor(QK[c % 2][:, :].rearrange("p (h d) -> p h d", d=DH),
                                RC[:, :].rearrange("p (h d) -> p h d", d=DH),
                                bc(DEC[:, c, :], 2, DH), ALU.mult).then_inc(s_qk, 1)

            def core(g, c, hb, k0):
                q = g.at * GT + c
                u = k0
                dve.wait_ge(s_tr[u % 2], hb + u // 2 + 1)
                v.tensor_tensor(DS[:, :, :], T[u % 2][:, 0:16 * VW].rearrange("p (a n) -> p a n", a=2), block2,
                                ALU.mult).then_inc(s_tf[u % 2], 1)
                for b in range(4):
                    u = k0 + 1 + b
                    dve.wait_ge(s_tr[u % 2], hb + u // 2 + 1)
                    dve.wait_ge(s_av, q * 4 + b + 7)
                    v.tensor_tensor(AM[b % 2][:, :, :], T[u % 2][:, :].rearrange("p (h t) -> p h t", h=4),
                                    bc(CN[:, C_CAUSAL:C_CAUSAL + P], 1, 4), ALU.mult).then_inc(s_tf[u % 2], 1)
                v.tensor_tensor(DS[:, :, :], S[:, :, :], DS[:, :, :], ALU.add)
                settle()
                dve.wait_ge(s_inter, q + 1)
                for a in range(2):
                    last = v.tensor_scalar(S[:, a, :], DS[:, a, :], PT[:, a, c:c + 1], None, ALU.mult)
                last.then_inc(s_st, 1)
                dve.wait_ge(s_av, q * 4 + 12)
                o = T2[:, 0:HEADS * VW].rearrange("p (h d) -> p h d", d=VW)
                v.tensor_scalar(DN[:, :], o[:, :, DH], DEN_EPS, None, ALU.add)
                settle()
                v.reciprocal(RD[:, :], DN[:, :])
                settle()
                v.tensor_tensor(Y[:, :, :], o[:, :, 0:DH], bc(RD[:, :], 2, DH), ALU.mult).then_inc(s_or, 1)

            def wo(g, c, hb, k0):
                q = g.at * GT + c
                dve.wait_ge(s_yhi, q + 1)
                v.tensor_tensor(YT[1][:, :, :], T[k0 % 2][:, 0:D].rearrange("p (k t) -> p k t", k=KD),
                                YT[0][:, :, :].bitcast(F32), ALU.subtract).then_inc(s_tf[k0 % 2], 1)
                u = k0 + 1
                dve.wait_ge(s_boa, g.at + 1)
                dve.wait_ge(s_tr[u % 2], hb + u // 2 + 1)
                xv = X[:, g.x + c, :]
                v.tensor_tensor(xv, T[u % 2][:, 0:D], xv, ALU.add).then_inc(s_tf[u % 2], 1)

            def do(step, *a):
                if step == "norm":
                    norm(*a)
                elif step == "ffn":
                    ffn(*a)
                elif step == "tail_b":
                    tail_b(*a)
                elif step == "proj":
                    proj(*a)
                elif step == "core":
                    core(*a)
                elif step == "wo":
                    wo(*a)

            v.sem_inc(s_st, 1)
            v.sem_inc(s_or, 1)
            run(dve, do)

        @block.tensor
        def _(pe):
            mm = nc.tensor.matmul
            PASSES = ((0, 0), (0, 1), (1, 0))

            def fresh(u, hb):
                need(pe, s_tf[u % 2], hb + u // 2)

            def taken(u, hb):
                pe.wait_ge(s_tf[u % 2], hb + u // 2 + 1)

            def norm(kind, r, g, hb, k0, prev, f):
                pe.wait_ge(s_xn, r + 1)
                for k in range(KD):
                    u = k0 + k
                    fresh(u, hb)
                    for c in range(GT):
                        last = nc.tensor.transpose(T[u % 2][:, c * P:(c + 1) * P], XN[:, c, k * P:(k + 1) * P], ident)
                    last.then_inc(s_tr[u % 2], 1)
                for k in range(KD):
                    taken(k0 + k, hb)
                u = k0 + 2
                fresh(u, hb)
                if kind == "A":
                    n = 0
                    for k in range(KD):
                        for a, b in PASSES:
                            last = mm(T[u % 2][0:HEADS, :], WP[b][:, k, 3 * D:QKV], XT[kind][a][:, k, :],
                                      start=n == 0, stop=n == 3 * KD - 1)
                            n += 1
                    last.then_inc(s_tr[u % 2], 1)
                    u = k0 + 3
                    pe.wait_ge(s_dp, g.at + 1)
                    fresh(u, hb)
                    ends = DP[:, :].rearrange("h (c t) -> h c t", c=GT)[:, :, P - 1]
                    for a in range(2):
                        mm(T[u % 2][:, P + a * GT:P + (a + 1) * GT], expand[:, a, :], ends, start=True, stop=True)
                    for c in range(GT):
                        for a, src in enumerate((DP, BT)):
                            at = c * 2 * HEADS + a * HEADS
                            last = nc.tensor.transpose(T[u % 2][:, at:at + HEADS], src[:, c * P:(c + 1) * P],
                                                CN[0:HEADS, C_ID:C_ID + HEADS])
                    last.then_inc(s_tr[u % 2], 1)
                else:
                    for c in range(GT):
                        n = 0
                        for k in range(KD):
                            for a, b in PASSES:
                                last = mm(T[u % 2][:, c * NR:(c + 1) * NR], XT[kind][a][:, k, c * P:(c + 1) * P],
                                          WR[b][:, k, :], start=n == 0, stop=n == 3 * KD - 1)
                                n += 1
                    last.then_inc(s_tr[u % 2], 1)
                    u = k0 + 3
                    pe.wait_ge(s_comb, f + 1)
                    fresh(u, hb)
                    for c in range(GT):
                        last = nc.tensor.transpose(T[u % 2][0:2 * NR, c * P:(c + 1) * P], CHL[:, c, :], ident)
                    last.then_inc(s_tr[u % 2], 1)

            def down(n, j):
                h = HID - j * P if j == FT - 1 else P
                m = n * FT + j
                pe.wait_ge(s_hl, m + 1)
                if j == 0:
                    need(pe, s_yr, n)
                for t in range(GT):
                    for i, (a, b) in enumerate(PASSES):
                        last = mm(PY[t // 2][:, (t % 2) * D:(t % 2 + 1) * D], (HH, HL)[a][j % 2][0:h, t * P:(t + 1) * P],
                                  WD[b][0:h, j, :], start=(j == 0 and i == 0 and t % 2 == 0),
                                  stop=(j == FT - 1 and i == 2), skip_group_check=True)
                last.then_inc(s_down, 1)

            def ffn(kind, n, j):
                h = HID - j * P if j == FT - 1 else P
                m = n * FT + j
                col = slice(j * P, j * P + h)
                if j == 0:
                    pe.wait_ge(s_ct, n + 1)
                need(pe, s_cbs, m)
                mm(PC[0:h, :], SEL[:, col], CT[kind][:, :], start=True, stop=True).then_inc(s_cb, 1)
                for w, out, free, ready in ((WG, PG, s_s, s_g), (WU, PU, s_w, s_u)):
                    need(pe, free, m)
                    i = 0
                    for k in range(KD):
                        for a, b in PASSES:
                            last = mm(out[0:h, :], w[b][:, k, col], XT[kind][a][:, k, :], start=i == 0, stop=i == 3 * KD - 1)
                            i += 1
                    last.then_inc(ready, 1)
                if j >= 2:
                    down(n, j - 2)

            def proj(g, c, hb, k0):
                for u, n0, n1 in ((k0, 0, 2 * D), (k0 + 1, 2 * D, 3 * D)):
                    fresh(u, hb)
                    i = 0
                    for k in range(KD):
                        for a, b in PASSES:
                            last = mm(T[u % 2][:, 0:n1 - n0], XT["A"][a][:, k, c * P:(c + 1) * P], WP[b][:, k, n0:n1],
                                      start=i == 0, stop=i == 3 * KD - 1)
                            i += 1
                    last.then_inc(s_tr[u % 2], 1)

            def turn(g, c, hb, k0):
                q = g.at * GT + c
                pe.wait_ge(s_qk, q + 1)
                fresh(k0, hb)
                for b in range(4):
                    last = nc.tensor.transpose(T[k0 % 2][:, b * P:(b + 1) * P], QK[c % 2][:, b * P:(b + 1) * P], ident)
                last.then_inc(s_tr[k0 % 2], 1)

            def core(g, c, hb, k0):
                q = g.at * GT + c
                va = VA[c % 2]
                taken(k0 - 2, hb)
                taken(k0 - 1, hb)
                pe.wait_ge(s_st, q + 1)
                pe.wait_ge(s_or, q + 1)
                for a in range(2):
                    last = mm(T2[:, a * 8 * VW:(a + 1) * 8 * VW], QT[:, a, :], S[:, a, :], start=a == 0, stop=False,
                              skip_group_check=True)
                last.then_inc(s_inter, 1)
                fresh(k0, hb)
                for a in range(2):
                    last = mm(T[k0 % 2][:, a * 8 * VW:(a + 1) * 8 * VW], QK[c % 2][:, D + a * P:D + (a + 1) * P],
                              va[:, 8 * a:8 * a + 8, :], start=True, stop=True)
                last.then_inc(s_tr[k0 % 2], 1)

                def values(b):
                    taken(k0 + 1 + b, hb)
                    for i in range(4):
                        hd = 8 * (i // 2) + 2 * b + i % 2
                        last = mm(T2[:, hd * VW:(hd + 1) * VW], AM[b % 2][:, i, :], va[:, hd, :], start=False,
                                  stop=hd == HEADS - 1, skip_group_check=True)
                    last.then_inc(s_av, 1)

                for b in range(4):
                    u = k0 + 1 + b
                    fresh(u, hb)
                    row = 32 * b
                    for i in range(4):
                        last = mm(T[u % 2][:, i * P:(i + 1) * P], KT[i % 2][row:row + 32, i // 2, :],
                                  QT[row:row + 32, i // 2, :], start=True, stop=True)
                    last.then_inc(s_tr[u % 2], 1)
                    if b > 0:
                        values(b - 1)
                values(3)

            def wo(g, c, hb, k0):
                q = g.at * GT + c
                pe.wait_ge(s_or, q + 2)
                fresh(k0, hb)
                yv = Y[:, :, :].rearrange("p h d -> p (h d)")
                for k in range(KD):
                    last = nc.tensor.transpose(T[k0 % 2][:, k * P:(k + 1) * P], yv[:, k * P:(k + 1) * P], ident)
                last.then_inc(s_tr[k0 % 2], 1)
                taken(k0, hb)
                u = k0 + 1
                fresh(u, hb)
                i = 0
                for k in range(KD):
                    for a, b in PASSES:
                        last = mm(T[u % 2][:, 0:D], YT[a][:, k, :], WO[b][:, k, :], start=i == 0, stop=i == 3 * KD - 1)
                        i += 1
                last.then_inc(s_tr[u % 2], 1)

            def do(step, *a):
                if step == "norm":
                    norm(*a)
                elif step == "ffn":
                    ffn(*a)
                elif step == "tail_a":
                    down(a[0], FT - 2)
                elif step == "tail_b":
                    down(a[0], FT - 1)
                elif step == "proj":
                    proj(*a)
                elif step == "turn":
                    turn(*a)
                elif step == "core":
                    core(*a)
                elif step == "wo":
                    wo(*a)

            pe.sem_inc(s_av, 8)
            pe.wait_ge(s_const, 16)
            pe.wait_ge(s_wready, 1)
            pe.wait_ge(s_lo, sum(splits))
            run(pe, do)


_INS = ["L0_attn_x", "L0_attn_Wq", "L0_attn_Wk", "L0_attn_Wv", "L0_attn_Wg", "L0_attn_bg", "L0_attn_Wo", "L0_attn_bo",
        "L0_ffn_gate_w", "L0_ffn_w_gate", "L0_ffn_w_up", "L0_ffn_w_down", "L0_ffn_shgate_w", "L0_ffn_shw_gate",
        "L0_ffn_shw_up", "L0_ffn_shw_down"]


def kernel(**inputs):
    import concourse.bacc as _bacc
    from concourse.bass_utils import run_bass_kernel_spmd as _run

    nc = _bacc.Bacc("TRN2", target_bir_lowering=False, num_devices=1)
    arrays, args = {}, []
    for name in _INS:
        a = np.ascontiguousarray(inputs[name])
        arrays[f"in_{name}"] = a
        args.append(nc.dram_tensor(f"in_{name}", a.shape, mybir.dt.from_np(a.dtype), kind="ExternalInput").ap())
    c = constants()
    arrays["in_constants"] = c
    args.append(nc.dram_tensor("in_constants", c.shape, F32, kind="ExternalInput").ap())
    c = selector()
    arrays["in_selector"] = c
    args.append(nc.dram_tensor("in_selector", c.shape, F32, kind="ExternalInput").ap())
    args.append(nc.dram_tensor("out", (B, L, D), F32, kind="ExternalOutput").ap())
    build(nc, *args)
    r = _run(nc, [arrays], core_ids=[0])
    return r.results[0]["out"]
```

```python
import concourse.bass as bass
from concourse import mybir
from collections import namedtuple
from contextlib import ExitStack
import numpy as np

F32 = mybir.dt.float32
F32R = mybir.dt.float32r
U32 = mybir.dt.uint32
ALU = mybir.AluOpType
ACT = mybir.ActivationFunctionType
AX = mybir.AxisListType

B, L, D = 4, 1024, 256
HEADS, DH = 16, 16
E, HE, HS = 8, 176, 352
P = 128
KD = D // P
GT = 4
GN = GT * P
NT = B * L // P
NG = NT // GT
XR = 4
STAGE = 7 * D
HID = E * HE + HS
FT = -(-HID // P)
HE_ALL = E * HE
NR = E + 2
VW = DH + 2
QKV = 3 * D + HEADS
LN_EPS, DEN_EPS = 1e-5, 1e-6
BETA_MIN, BETA_MAX = 0.8, 0.9995

C_ID = 0
C_CAUSAL = C_ID + P
C_BLOCK = C_CAUSAL + P
C_ROPE = C_BLOCK + 8 * VW
C_PAR = C_ROPE + NT * 16
C_IOTA = C_PAR + 2
C_KEEP = C_IOTA + E
C_EXP = C_KEEP + NT
C_HALF = C_EXP + 2 * P
C_ALL = C_HALF + GT

PARTS = ((0, 3), (3, 6), (6, E))
PART_AT = tuple(a * HE // P for a, _ in PARTS)


def constants():
    c = np.zeros((P, C_ALL), np.float32)
    p = np.arange(P)
    c[:, C_ID:C_ID + P] = np.eye(P)
    c[:, C_CAUSAL:C_CAUSAL + P] = p[:, None] <= p[None, :]
    c[:, C_BLOCK:C_BLOCK + 8 * VW] = (p[:, None] // DH) == (np.arange(8 * VW)[None, :] // VW)
    half = DH // 2
    inv = (np.float32(1.0) / np.float32(10000.0) ** (np.arange(half, dtype=np.float32) / np.float32(half))).astype(np.float32)
    ang = (np.arange(L, dtype=np.float32)[:, None] * inv[None, :]).astype(np.float32)
    tab = np.concatenate([np.cos(ang), np.sin(ang)], 1).astype(np.float32)
    tab = tab.reshape(L // P, P, 16).transpose(1, 0, 2)
    c[:, C_ROPE:C_ROPE + NT * 16] = np.tile(tab, (1, B, 1)).reshape(P, NT * 16)
    c[:, C_PAR] = (p // DH) % 2 == 0
    c[:, C_PAR + 1] = (p // DH) % 2 == 1
    c[:, C_IOTA:C_IOTA + E] = np.arange(E)
    c[:, C_KEEP:C_KEEP + NT] = (np.arange(NT) % (L // P)) != L // P - 1
    for h in range(HEADS):
        c[h, C_EXP + h * DH:C_EXP + (h + 1) * DH] = 1.0
    c[:, C_HALF:C_HALF + GT] = -0.5
    return c


def selector():
    c = np.zeros((2 * NR, HID), np.float32)
    for r in (0, NR):
        for e in range(E + 1):
            c[r + e, e * HE:(e + 1) * HE if e < E else HID] = 1.0
    return c


Group = namedtuple("Group", "at x")


def group(g):
    return Group(g, g % XR * GT)


def need(eng, sem, value):
    if not isinstance(value, int) or value > 0:
        eng.wait_ge(sem, value)


def bc(ap, axis, n):
    v = ap.unsqueeze(axis)
    s = list(v.shape)
    s[axis] = n
    return v.broadcast_to(s)


USES = {"proj": 2, "turn": 1, "core": 2, "core_1": 1, "core_2": 1, "core_3": 1, "wo_turn": 1, "wo": 1,
        "norm_turn": 2, "norm_first": 1, "norm_last": 1}
U_FIRST = 2 * 4
U_SECOND = 2 * 4 + 2 * 10
U_LOOP = 3 * 4 + GT * 10

NORM = (("norm_stats", 0), ("norm_var", 1), ("norm_scale", 1), ("norm_turn", 2), ("norm_first", 1), ("norm_mid", 2), ("norm_last", 2))
CHUNK = (("proj", 0), ("phi", 1), ("turn", 2), ("core", 1), ("core_1", 1), ("core_2", 1), ("core_3", 1), ("core_4", 1),
         ("attend", 0), ("wo_turn", 1), ("wo", 1))
Norm = namedtuple("Norm", "kind buf r g f prev")


def slots(norms, chunks):
    out = {}
    for at, norm in norms:
        for step, gap in NORM:
            at += gap
            out.setdefault(at, []).append([step, norm])
    for at, g, c in chunks:
        for step, gap in CHUNK:
            at += gap
            out.setdefault(at, []).append([step, g, c])
    for steps in out.values():
        steps.sort(key=lambda s: s[0] in ("norm_stats", "norm_var", "norm_scale"))
    return out


def ordered(hb, table, tiles, tails):
    k = 0
    own = {}
    for half in range(max([*table, *[2 * t + 1 for t in [*tiles, *tails]]]) + 1):
        slot = half // 2
        if half % 2 == 0 and slot in tiles:
            yield ("ffn", *tiles[slot])
        if half % 2:
            yield from tails.get(slot, ())
            if slot in tiles and tiles[slot][2] >= 2:
                yield ("down", tiles[slot][1], tiles[slot][2] - 2)
        for step, who, *c in table.get(half, ()):
            mine = own.setdefault((id(who), *c), {})
            if step in USES:
                mine[step] = k
                k += USES[step]
            yield (step, who, *c, hb, dict(mine))


def tiles_at(slot, buf, n):
    return {slot + j: (buf, n, j) for j in range(FT)}


def tails_at(slot, n, g, final):
    return {slot: [("tail_a", n)], slot + 1: [("tail_b", n, g, final)]}


CH = 7


def first():
    norm = Norm("F1", 0, 0, group(0), 0, None)
    yield ("split", 0)
    for s in ordered(0, slots([(0, norm)], []), {}, {}):
        if s[0] == "norm_first":
            yield ("split", 1)
        yield s
    splits = {0: [("split", 2)], PART_AT[1]: [("split", 3)], 2 * PART_AT[1]: [("split", 4)]}
    yield from ordered(2, slots([(13, Norm("F1", 1, 1, group(1), 1, None))], []), tiles_at(0, 0, 0), splits)


def second():
    a0, f2 = Norm("A", "A", 2, group(0), None, 0), Norm("F1", 0, 3, group(2), 2, 0)
    yield from ordered(U_FIRST // 2, slots([(4, a0), (15, f2)], [(13 + CH * c, group(0), c) for c in range(2)]),
                       tiles_at(0, 1, 1), tails_at(0, 0, group(0), False))


def loop_base(i):
    return (i - 2) * (U_LOOP // 2) + (U_FIRST + U_SECOND) // 2


def middle(i, back3, back2, back1, this, ahead):
    norms = [(CH + 2, Norm("A", "A", 3 * i - 2, back1, None, i - 1)),
             (2 * CH + 4, Norm("F2", 1, 3 * i - 1, back2, 2 * i - 1, 2 * i - 3)),
             (32, Norm("F1", 0, 3 * i, ahead, 2 * i, 2 * i - 2))]
    chunks = [(0, back2, 2), (CH, back2, 3), (28, back1, 0), (42, back1, 1)]
    tiles = tiles_at(0, 0, 2 * i - 2) | tiles_at(FT, 1, 2 * i - 1)
    tails = tails_at(0, 2 * i - 3, back1 if back3 is None else back3, back3 is not None) | tails_at(FT, 2 * i - 2, this, False)
    yield from ordered(loop_base(i), slots(norms, chunks), tiles, tails)


def last():
    i = NG - 1
    g3, g2, g1, g0 = (group(i - k) for k in (3, 2, 1, 0))
    c1 = 2 * CH + 2
    c0 = c1 + 4 * CH + 2
    t1, t0 = 2 * FT + 1, 3 * FT + 3
    norms = [(c1 - 8, Norm("A", "A", 3 * i - 2, g1, None, i - 1)),
             (c1 + 2, Norm("F2", 1, 3 * i - 1, g2, 2 * i - 1, 2 * i - 3)),
             (c0 - 8, Norm("A", "A", 3 * i, g0, None, i)),
             (c1 + 4 * CH + 4, Norm("F2", 0, 3 * i + 1, g1, 2 * i, 2 * i - 2)),
             (c0 + 4 * CH + 4, Norm("F2", 1, 3 * i + 2, g0, 2 * i + 1, 2 * i - 1))]
    chunks = [(0, g2, 2), (CH, g2, 3)] + [(at + CH * c, g, c) for at, g in ((c1, g1), (c0, g0)) for c in range(GT)]
    tiles = tiles_at(0, 0, 2 * i - 2) | tiles_at(FT, 1, 2 * i - 1) | tiles_at(t1, 0, 2 * i) | tiles_at(t0, 1, 2 * i + 1)
    tails = (tails_at(0, 2 * i - 3, g3, True) | tails_at(FT, 2 * i - 2, g0, False) | tails_at(2 * FT, 2 * i - 1, g2, True)
             | tails_at(t1 + FT, 2 * i, g1, True) | tails_at(t0 + FT, 2 * i + 1, g0, True))
    yield from ordered(loop_base(i), slots(norms, chunks), tiles, tails)


def run(eng, parts):
    def do(step, *a):
        if step in parts:
            parts[step](*a)

    for s in [*first(), *second(), *middle(2, None, *(group(g) for g in range(4)))]:
        do(*s)
    with eng.Fori(3, NG - 1) as i:
        gs = [Group(i + k, eng.snap((i + k) % XR * GT)) for k in (-3, -2, -1, 0, 1)]
        for s in middle(i, *gs):
            do(*s)
    for s in last():
        do(*s)


def build(nc, x_d, wq_d, wk_d, wv_d, wg_d, bg_d, wo_d, bo_d, gw_d, eg_d, eu_d, ed_d, sgw_d, sg_d, su_d, sd_d, c_d, sel_d, out_d):
    ctx = ExitStack()
    with ctx:
        def sb(name, shape, dt=F32):
            return ctx.enter_context(nc.sbuf_tensor(name, shape, dt))

        def pb(name):
            return ctx.enter_context(nc.psum_tensor(name, [P, 512], F32))

        def sem(name):
            return ctx.enter_context(nc.semaphore(name))

        X = sb("X", [P, XR * GT, D])
        CN = sb("CN", [P, C_ALL])
        SEL = sb("SEL", [2 * NR, HID], F32R)
        WG = [sb(f"WG{k}", [P, KD, HID], F32R) for k in "hl"]
        WU = [sb(f"WU{k}", [P, KD, HID], F32R) for k in "hl"]
        WD = [sb(f"WD{k}", [P, FT, D], F32R) for k in "hl"]
        WP = [sb(f"WP{k}", [P, KD, QKV], F32R) for k in "hl"]
        WO = [sb(f"WO{k}", [P, KD, D], F32R) for k in "hl"]
        R32 = sb("R32", [P, KD, NR])
        WR = sb("WR", [P, KD, 2 * NR], F32R)
        BO = sb("BO", [P, D])
        HBG = sb("HBG", [HEADS, 1])
        ST = sb("ST", [P, GT, 6])
        MV = sb("MV", [P, GT, 2])
        XN = sb("XN", [P, GT, D])
        VE = sb("VE", [P, GT])
        RS = sb("RS", [P, GT])
        XT = {k: [sb(f"XT{k}{h}", [P, KD, GN], F32R) for h in "hl"] for k in (0, 1, "A")}
        LG = sb("LG", [P, GT, NR])
        TOP = sb("TOP", [P, GT, 8])
        IDX = sb("IDX", [P, GT, 8], U32)
        IDF = sb("IDF", [P, GT, 2])
        GAP = sb("GAP", [P, GT])
        E2 = sb("E2", [P, GT])
        SGT = sb("SGT", [P, GT])
        DEN2 = sb("DEN2", [P, GT])
        W12 = sb("W12", [P, 2, GT])
        HOT = sb("HOT", [P, 2, GT, E])
        CMB = sb("CMB", [P, GT, NR])
        CHL = sb("CHL", [P, GT, 2 * NR])
        CT = {k: sb(f"CT{k}", [2 * NR, GN], F32R) for k in range(2)}
        CBS = [sb(f"CBS{k}", [P, GN]) for k in range(2)]
        TH = [sb(f"TH{k}", [P, GN]) for k in range(2)]
        HH = [sb(f"HH{k}", [P, GN], F32R) for k in range(2)]
        HL = [sb(f"HL{k}", [P, GN], F32R) for k in range(2)]
        BT = sb("BT", [HEADS, GN])
        ZR = sb("ZR", [HEADS, P])
        DP = sb("DP", [HEADS, GN])
        DEC = sb("DEC", [P, GT, 2 * HEADS])
        PT = sb("PT", [P, 2, GT])
        SCRATCH = sb("SCRATCH", [P, 2 * STAGE])
        STG = [SCRATCH[:, k * STAGE:(k + 1) * STAGE] for k in range(2)]
        RC, RT, QK0, QK1 = (SCRATCH[:, k * 2 * D:(k + 1) * 2 * D] for k in range(4))
        QK = [QK0, QK1]
        AM1 = SCRATCH[:, 8 * D:10 * D].rearrange("p (h t) -> p h t", h=4)
        VA = [sb(f"VA{k}", [P, HEADS, VW]) for k in range(2)]
        QT, KT0, KT1 = (SCRATCH[:, (10 + k) * D:(11 + k) * D].rearrange("p (a t) -> p a t", a=2) for k in range(3))
        KT = [KT0, KT1]
        AM = [sb("AM0", [P, 4, P]), AM1]
        S = sb("S", [P, 2, 8 * VW])
        DS = sb("DS", [P, 2, 8 * VW])
        DN = sb("DN", [P, HEADS])
        RD = sb("RD", [P, HEADS])
        Y = sb("Y", [P, HEADS, DH])
        YT = [sb(f"YT{k}", [P, KD, P], F32R) for k in "hl"]

        T = [pb(f"T{k}") for k in range(2)]
        T2 = pb("T2")
        PG, PU, PC = pb("PG"), pb("PU"), pb("PC")
        PY = [pb(f"PY{k}") for k in range(2)]

        ident = CN[:, C_ID:C_ID + P]
        rope = CN[:, C_ROPE:C_ROPE + NT * 16].rearrange("p (t c) -> p t c", c=16)
        expand = CN[0:HEADS, C_EXP:C_EXP + 2 * P].rearrange("p (a c) -> p a c", a=2)
        block2 = bc(CN[:, C_BLOCK:C_BLOCK + 8 * VW], 1, 2)

        s_const, s_x0, s_x1, s_xrest, s_small, s_bo = (sem(n) for n in (
            "const_loaded", "x0_loaded", "x1_loaded", "xrest_loaded", "router_loaded", "bo_loaded"))
        s_stage = [sem(f"stage{k}_loaded") for k in range(2)]
        s_hi, s_lo, s_prep, s_wready = sem("weight_high"), sem("weight_low"), sem("prepared"), sem("weights_ready")
        s_tr = [sem(f"tmp{k}_ready") for k in range(2)]
        s_tf = [sem(f"tmp{k}_free") for k in range(2)]
        s_var, s_rstd, s_xn, s_xh = sem("var"), sem("rstd"), sem("xn"), sem("xt_high")
        s_gap, s_e2, s_comb, s_ct = sem("gap"), sem("top2_exp"), sem("comb"), sem("comb_turned")
        s_cb, s_cbs, s_g, s_th, s_u, s_w, s_s = (sem(n) for n in (
            "comb_spread", "comb_copied", "gate", "gate_tanh", "up", "up_weighted", "gate_silu"))
        s_h, s_hh, s_hl, s_down, s_yr = (sem(n) for n in (
            "hidden", "hidden_high", "hidden_low", "down", "y_added"))
        s_dp, s_dec, s_boa = sem("decay"), sem("decay_turned"), sem("bo_added")
        s_rt, s_ro, s_mn, s_ex, s_qk = (sem(n) for n in (
            "rope_parts", "rope_sum", "phi_min", "phi_exp", "qk_scaled"))
        s_inter, s_or, s_st = (sem(n) for n in ("inter", "core_read", "state"))
        s_av, s_yhi, s_out, s_store = sem("scores_used"), sem("attn_y_high"), sem("out_ready"), sem("stored")

        xt_view = x_d.rearrange("b (t p) d -> p (b t) d", p=P)
        ot_view = out_d.rearrange("b (t p) d -> p (b t) d", p=P)
        block = ctx.enter_context(nc.Block())

        def kcols(w, k):
            return w[k * P:(k + 1) * P, :]

        def hidden_piece(w, s, dst, a, b):
            n = (b - a) * HE
            full = n + (HS if b == E else 0)
            ld = []
            for k in range(KD):
                ld.append(((P, k * full, k * full + n, b - a), w[a:b, k * P:(k + 1) * P, :].rearrange("e p h -> p e h")))
                if b == E:
                    ld.append(((P, k * full + n, (k + 1) * full, 0), kcols(s, k)))
            return ld, [(P, 0, KD * full, dst[0][:, :, a * HE:a * HE + full], dst[1][:, :, a * HE:a * HE + full])]

        edf = ed_d.rearrange("e h d -> (e h) d")

        def down_piece(t0, t1):
            if t1 * P <= HE_ALL:
                return ([((P, 0, (t1 - t0) * D, t1 - t0), edf[t0 * P:t1 * P, :].rearrange("(t p) d -> p t d", p=P))],
                        [(P, 0, (t1 - t0) * D, WD[0][:, t0:t1, :], WD[1][:, t0:t1, :])])
            ne, ns = HE_ALL // P - t0, HS // P
            rest = HS - ns * P
            m = ne + ns
            return ([((P, 0, ne * D, ne), edf[t0 * P:HE_ALL, :].rearrange("(t p) d -> p t d", p=P)),
                     ((P, ne * D, m * D, ns), sd_d[0:ns * P, :].rearrange("(t p) d -> p t d", p=P)),
                     ((rest, m * D, (m + 1) * D, 0), sd_d[ns * P:HS, :])],
                    [(P, 0, m * D, WD[0][:, t0:t0 + m, :], WD[1][:, t0:t0 + m, :]),
                     (rest, m * D, (m + 1) * D, WD[0][0:rest, t0 + m, :], WD[1][0:rest, t0 + m, :])])

        pieces, batch = [([((2 * NR, 0, HID, 0), sel_d)], [(2 * NR, 0, HID, SEL[:, :], None)])], [1]
        for n, (a, b) in enumerate(PARTS):
            pieces += [hidden_piece(eg_d, sg_d, WG, a, b), hidden_piece(eu_d, su_d, WU, a, b),
                       down_piece(PART_AT[n], PART_AT[n + 1] if b < E else FT)]
            batch.append(3)
        batch.append(2)
        loads = [((P, k * QKV + w * D, k * QKV + w * D + m.shape[1], 0), kcols(m, k))
                 for w, m in enumerate((wq_d, wk_d, wv_d, wg_d)) for k in range(KD)]
        pieces.append((loads, [(P, 0, KD * QKV, WP[0][:, :, :], WP[1][:, :, :])]))
        pieces.append(([((P, 0, KD * D, KD), wo_d.rearrange("(k p) n -> p k n", p=P))],
                       [(P, 0, KD * D, WO[0][:, :, :], WO[1][:, :, :])]))
        staged = [0, 0]
        arrive = []
        for k, (ld, _) in enumerate(pieces):
            staged[k % 2] += 16 * len(ld)
            arrive.append(staged[k % 2])
        splits = [len(c) for _, c in pieces]

        def pieces_of(part):
            p0 = sum(batch[:part])
            return [(k, sum(splits[:k]), pieces[k][1]) for k in range(p0, p0 + batch[part])]

        def shaped(ap, like):
            if len(like.shape) == 2:
                return ap
            return ap.rearrange("p (a b) -> p a b", a=like.shape[1])

        @block.sync
        def _(sp):
            sp.dma_start(X[:, 0:GT, :], xt_view[:, 0:GT, :]).then_inc(s_x0, 16)
            sp.dma_start(CN[:, :], c_d).then_inc(s_const, 16)
            for k, (ld, _) in enumerate(pieces):
                if k >= 2:
                    sp.wait_ge(s_lo, sum(splits[:k - 1]))
                for (rows, a, b, t), src in ld:
                    dst = STG[k % 2][0:rows, a:b]
                    if t:
                        dst = dst.rearrange("p (t n) -> p t n", t=t)
                    sp.dma_start(dst, src).then_inc(s_stage[k % 2], 16)
                if k == 6:
                    sp.dma_start(X[:, GT:2 * GT, :], xt_view[:, GT:2 * GT, :]).then_inc(s_x1, 16)
            sp.dma_start(BO[:, :], bo_d.rearrange("(a n) -> a n", a=1).broadcast_to([P, D])).then_inc(s_bo, 16)
            sp.dma_start(X[:, 2 * GT:3 * GT, :], xt_view[:, 2 * GT:3 * GT, :]).then_inc(s_xrest, 16)
            sp.wait_ge(s_xrest, 16)
            sp.dma_start(X[:, 3 * GT:4 * GT, :], xt_view[:, 3 * GT:4 * GT, :]).then_inc(s_xrest, 16)
            for g in range(NG):
                at = g % XR * GT
                sp.wait_ge(s_out, g + 1)
                sp.dma_start(ot_view[:, g * GT:(g + 1) * GT, :], X[:, at:at + GT, :]).then_inc(s_store, 16)
                if g + XR < NG:
                    sp.wait_ge(s_store, 16 * g + 16)
                    sp.wait_ge(s_xrest, 16 * g + 32)
                    sp.dma_start(X[:, at:at + GT, :], xt_view[:, (g + XR) * GT:(g + XR + 1) * GT, :]).then_inc(s_xrest, 16)
            sp.wait_ge(s_store, 16 * NG)

        @block.gpsimd
        def _(pool):
            pool.wait_ge(s_prep, 1)
            with nc.allow_non_contiguous_dma("router columns"):
                for k in range(KD):
                    pool.dma_start(R32[:, k, 0:E], gw_d[:, k * P:(k + 1) * P].rearrange("e p -> p e")).then_inc(s_small, 16)
                    pool.dma_start(R32[:, k, E:E + 1], sgw_d[k * P:(k + 1) * P].rearrange("(p a) -> p a", a=1)).then_inc(s_small, 16)
                pool.dma_start(HBG[:, :], bg_d.rearrange("(p a) -> p a", a=1)).then_inc(s_small, 16)
            for k in range(2):
                nc.gpsimd.memset(VA[k][:, :, :], 1.0)
            nc.gpsimd.memset(S[:, :, :], 0.0)
            nc.gpsimd.memset(CMB[:, :, :], 0.0)
            nc.gpsimd.memset(ZR[:, :], 0.0).then_inc(s_prep, 1)
            pool.wait_ge(s_const, 16)

            def low(m, j):
                h = HID - j * P if j == FT - 1 else P
                pool.wait_ge(s_hh, m + 1)
                need(pool, s_down, m - 1)
                nc.gpsimd.tensor_tensor(HL[j % 2][0:h, :], TH[j % 2][0:h, :], HH[j % 2][0:h, :].bitcast(F32),
                                        ALU.subtract).then_inc(s_hl, 1)

            def norm_var(norm, hb, u):
                pool.wait_ge(s_var, norm.r + 1)
                nc.gpsimd.tensor_tensor(RS[:, :], VE[:, :], CN[:, C_HALF:C_HALF + GT], ALU.pow).then_inc(s_rstd, 1)

            def norm_scale(norm, hb, u):
                if norm.kind == "A":
                    pool.wait_ge(s_xn, norm.r + 1)
                    pool.wait_ge(s_bo, 16)
                    v = X[:, bass.ds(norm.g.x, GT), :]
                    nc.gpsimd.tensor_tensor(v, v, bc(BO[:, :], 1, GT), ALU.add).then_inc(s_boa, 1)

            def ffn(buf, n, j):
                h = HID - j * P if j == FT - 1 else P
                m = n * FT + j
                if j > 0:
                    low(m - 1, j - 1)
                pool.wait_ge(s_s, m + 1)
                pool.wait_ge(s_w, m + 1)
                nc.gpsimd.tensor_tensor(TH[j % 2][0:h, :], TH[j % 2][0:h, :], CBS[j % 2][0:h, :], ALU.mult).then_inc(s_h, 1)

            def proj(g, c, hb, u):
                pool.wait_ge(s_rt, g.at * GT + c + 1)
                nc.gpsimd.tensor_tensor(RC[:, :], RC[:, :], RT[:, :], ALU.add).then_inc(s_ro, 1)

            def tail_a(n):
                low(n * FT + FT - 1, FT - 1)

            pool.sem_inc(s_ro, 1)
            run(pool, {"norm_var": norm_var, "norm_scale": norm_scale, "ffn": ffn, "proj": proj, "tail_a": tail_a})

        @block.scalar
        def _(act):
            act.wait_ge(s_const, 16)
            act.wait_ge(s_small, 80)
            nc.scalar.activation(WR[:, :, 0:NR], R32[:, :, :], ACT.Copy).then_inc(s_hi, 1)

            def split(part):
                for k, _, cuts in pieces_of(part):
                    act.wait_ge(s_stage[k % 2], arrive[k])
                    for rows, a, b, hi, lo in cuts:
                        nc.scalar.activation(hi, shaped(STG[k % 2][0:rows, a:b], hi), ACT.Copy).then_inc(s_hi, 1)

            def copy_high(m, j):
                h = HID - j * P if j == FT - 1 else P
                act.wait_ge(s_h, m + 1)
                need(act, s_down, m - 1)
                nc.scalar.activation(HH[j % 2][0:h, :], TH[j % 2][0:h, :], ACT.Copy).then_inc(s_hh, 1)

            def ready(u, hb):
                act.wait_ge(s_tr[u % 2], hb + u // 2 + 1)

            def norm_turn(norm, hb, u):
                for k in range(KD):
                    n = u["norm_turn"] + k
                    ready(n, hb)
                    if k == 0 and norm.prev is not None:
                        if norm.kind == "A":
                            need(act, s_qk, norm.prev * GT)
                        else:
                            act.wait_ge(s_u, norm.prev * FT + FT)
                    nc.scalar.activation(XT[norm.buf][0][:, k, :], T[n % 2][:, :], ACT.Copy).then_inc(s_xh, 1)

            def norm_first(norm, hb, u):
                if norm.kind == "A":
                    n = u["norm_first"]
                    ready(n, hb)
                    nc.scalar.activation(BT[:, :], T[n % 2][0:HEADS, :], ACT.Tanh, bias=HBG[:, 0:1],
                                         scale=0.5).then_inc(s_tf[n % 2], 1)
                else:
                    act.wait_ge(s_gap, norm.f + 1)
                    nc.scalar.activation(E2[:, :], GAP[:, :], ACT.Exp)
                    nc.scalar.activation(SGT[:, :], LG[:, :, E], ACT.Tanh, scale=0.5).then_inc(s_e2, 1)

            def norm_last(norm, hb, u):
                n = u["norm_last"]
                ready(n, hb)
                if norm.kind == "A":
                    nc.scalar.activation(DEC[:, :, 0:HEADS], T[n % 2][:, 0:GT * HEADS].rearrange("p (c h) -> p c h", c=GT),
                                         ACT.Copy).then_inc(s_dec, 1)
                else:
                    nc.scalar.activation(CT[norm.buf][:, :], T[n % 2][0:2 * NR, :], ACT.Copy).then_inc(s_tf[n % 2], 1)
                    act.wait_ge(s_tf[n % 2], hb + n // 2 + 1)
                    act.sem_inc(s_ct, 1)

            def ffn(buf, n, j):
                h = HID - j * P if j == FT - 1 else P
                m = n * FT + j
                act.wait_ge(s_cb, m + 1)
                need(act, s_h, m - 1)
                nc.scalar.activation(CBS[j % 2][0:h, :], PC[0:h, :], ACT.Copy).then_inc(s_cbs, 1)
                if j > 0:
                    copy_high(m - 1, j - 1)
                act.wait_ge(s_g, m + 1)
                need(act, s_hl, m - 1)
                nc.scalar.activation(TH[j % 2][0:h, :], PG[0:h, :], ACT.Tanh, scale=0.5).then_inc(s_th, 1)

            def proj(g, c, hb, u):
                q = g.at * GT + c
                n = u["proj"] + 1
                ready(n, hb)
                act.wait_ge(s_av, q * 4 + 4)
                nc.scalar.activation(VA[c % 2][:, :, 0:DH], T[n % 2][:, 0:D].rearrange("p (h d) -> p h d", h=HEADS),
                                     ACT.Copy).then_inc(s_tf[n % 2], 1)

            def phi(g, c, hb, u):
                act.wait_ge(s_mn, g.at * GT + c + 1)
                nc.scalar.activation(RT[:, :], RT[:, :], ACT.Exp).then_inc(s_ex, 1)

            def turn(g, c, hb, u):
                n = u["turn"]
                ready(n, hb)
                act.wait_ge(s_av, (g.at * GT + c) * 4 + 8)
                t = T[n % 2][:, :].rearrange("p (a b t) -> p a b t", a=2, b=2)
                nc.scalar.activation(QT[:, :, :], t[:, 0], ACT.Copy)
                nc.scalar.activation(KT[0][:, :, :], t[:, 1], ACT.Copy, scale=CN[:, C_PAR:C_PAR + 1])
                nc.scalar.activation(KT[1][:, :, :], t[:, 1], ACT.Copy, scale=CN[:, C_PAR + 1:C_PAR + 2]).then_inc(s_tf[n % 2], 1)

            def wo_turn(g, c, hb, u):
                n = u["wo_turn"]
                ready(n, hb)
                nc.scalar.activation(YT[0][:, :, :], T[n % 2][:, 0:D].rearrange("p (k t) -> p k t", k=KD),
                                     ACT.Copy).then_inc(s_yhi, 1)

            def tail_a(n):
                copy_high(n * FT + FT - 1, FT - 1)

            run(act, {"split": split, "norm_turn": norm_turn, "norm_first": norm_first, "norm_last": norm_last, "ffn": ffn,
                      "proj": proj, "phi": phi, "turn": turn, "wo_turn": wo_turn, "tail_a": tail_a})

        @block.vector
        def _(dve):
            v = nc.vector
            v.memset(R32[:, :, :], 0.0).then_inc(s_prep, 1)
            dve.wait_ge(s_small, 80)
            v.tensor_scalar(HBG[:, :], HBG[:, :], 0.5, None, ALU.mult)
            dve.wait_ge(s_hi, 1)
            v.tensor_tensor(WR[:, :, NR:2 * NR], R32[:, :, :], WR[:, :, 0:NR].bitcast(F32), ALU.subtract).then_inc(s_wready, 1)
            def settle():
                dve.drain()

            def split(part):
                for k, done, cuts in pieces_of(part):
                    for rows, a, b, hi, lo in cuts:
                        done += 1
                        dve.wait_ge(s_hi, done + 1)
                        if lo is None:
                            v.sem_inc(s_lo, 1)
                        else:
                            v.tensor_tensor(lo, shaped(STG[k % 2][0:rows, a:b], hi), hi.bitcast(F32),
                                            ALU.subtract).then_inc(s_lo, 1)

            def ready(u, hb):
                dve.wait_ge(s_tr[u % 2], hb + u // 2 + 1)

            def norm_stats(norm, hb, u):
                g = norm.g
                settle()
                if norm.kind == "F1":
                    if isinstance(g.at, int) and g.at == 0:
                        dve.wait_ge(s_x0, 16)
                        dve.wait_ge(s_const, 16)
                    elif isinstance(g.at, int) and g.at == 1:
                        dve.wait_ge(s_x1, 16)
                    else:
                        dve.wait_ge(s_xrest, 16 * g.at - 16)
                for c in range(GT):
                    v.bn_stats(ST[:, c, :], X[:, g.x + c, :])

            def norm_var(norm, hb, u):
                settle()
                for c in range(GT):
                    v.bn_aggr(MV[:, c, :], ST[:, c, :])
                settle()
                v.tensor_scalar(VE[:, :], MV[:, :, 1], LN_EPS, None, ALU.add).then_inc(s_var, 1)

            def norm_scale(norm, hb, u):
                dve.wait_ge(s_rstd, norm.r + 1)
                for c in range(GT):
                    last = v.tensor_scalar(XN[:, c, :], X[:, norm.g.x + c, :], MV[:, c, 0:1], RS[:, c:c + 1],
                                           ALU.subtract, ALU.mult)
                last.then_inc(s_xn, 1)

            def norm_turn(norm, hb, u):
                for k in range(KD):
                    n = u["norm_turn"] + k
                    dve.wait_ge(s_xh, norm.r * KD + k + 1)
                    v.tensor_tensor(XT[norm.buf][1][:, k, :], T[n % 2][:, :], XT[norm.buf][0][:, k, :].bitcast(F32),
                                    ALU.subtract).then_inc(s_tf[n % 2], 1)

            def norm_first(norm, hb, u):
                n = u["norm_first"]
                if norm.kind == "A":
                    dve.wait_ge(s_tf[n % 2], hb + n // 2 + 1)
                    v.tensor_scalar(BT[:, :], BT[:, :], 0.5, 0.5, ALU.mult, ALU.add)
                    settle()
                    v.tensor_scalar(BT[:, :], BT[:, :], BETA_MIN, BETA_MAX, ALU.max, ALU.min)
                    settle()
                    for c in range(GT):
                        t = slice(c * P, (c + 1) * P)
                        last = v.tensor_tensor_scan(DP[:, t], BT[:, t], ZR[:, :], 1.0, ALU.mult, ALU.add)
                    last.then_inc(s_dp, 1)
                    return
                ready(n, hb)
                t = T[n % 2][:, 0:GT * 2 * NR].rearrange("p (c a e) -> p c a e", c=GT, a=2)
                v.tensor_copy(LG[:, :, :], t[:, :, 1, :])
                settle()
                v.tensor_tensor(LG[:, :, :], t[:, :, 0, :], LG[:, :, :], ALU.add).then_inc(s_tf[n % 2], 1)
                settle()
                for c in range(GT):
                    v.max(TOP[:, c, :], LG[:, c, 0:E])
                settle()
                v.tensor_tensor(GAP[:, :], TOP[:, :, 1], TOP[:, :, 0], ALU.subtract).then_inc(s_gap, 1)
                for c in range(GT):
                    v.max_index(IDX[:, c, :], TOP[:, c, :], LG[:, c, 0:E])
                settle()
                v.tensor_copy(IDF[:, :, :], IDX[:, :, 0:2])
                settle()
                for k in range(2):
                    v.tensor_tensor(HOT[:, k], bc(CN[:, C_IOTA:C_IOTA + E], 1, GT), bc(IDF[:, :, k], 2, E), ALU.is_equal)

            def norm_mid(norm, hb, u):
                if norm.kind == "A":
                    return
                dve.wait_ge(s_e2, norm.f + 1)
                v.tensor_scalar(DEN2[:, :], E2[:, :], 4.0, 4.0, ALU.mult, ALU.add)
                v.tensor_scalar(CMB[:, :, E], SGT[:, :], 1.0, 0.125, ALU.add, ALU.mult)
                settle()
                v.reciprocal(W12[:, 0, :], DEN2[:, :])
                settle()
                v.tensor_tensor(W12[:, 1, :], W12[:, 0, :], E2[:, :], ALU.mult)
                settle()
                v.tensor_tensor(HOT[:, :, :, :], HOT[:, :, :, :], bc(W12[:, :, :], 3, E), ALU.mult)
                settle()
                v.tensor_tensor(CMB[:, :, 0:E], HOT[:, 0], HOT[:, 1], ALU.add)
                settle()
                v.tensor_copy(CHL[:, :, 0:NR].bitcast(F32R), CMB[:, :, :])
                settle()
                v.tensor_tensor(CHL[:, :, NR:2 * NR], CMB[:, :, :], CHL[:, :, 0:NR], ALU.subtract).then_inc(s_comb, 1)

            def norm_last(norm, hb, u):
                if norm.kind == "A":
                    n = u["norm_last"]
                    dve.wait_ge(s_dec, norm.g.at + 1)
                    ready(n, hb)
                    v.tensor_tensor(PT[:, :, :], T[n % 2][:, P:P + 2 * GT].rearrange("p (a c) -> p a c", a=2),
                                    bc(CN[:, bass.ds(norm.g.at * GT + C_KEEP, GT)], 1, 2), ALU.mult).then_inc(s_tf[n % 2], 1)
                    v.reciprocal(DEC[:, :, HEADS:2 * HEADS], DEC[:, :, 0:HEADS])

            def ffn(buf, n, j):
                h = HID - j * P if j == FT - 1 else P
                m = n * FT + j
                dve.wait_ge(s_th, m + 1)
                v.scalar_tensor_tensor(TH[j % 2][0:h, :], TH[j % 2][0:h, :], 1.0, PG[0:h, :], ALU.add, ALU.mult).then_inc(s_s, 1)
                dve.wait_ge(s_cbs, m + 1)
                dve.wait_ge(s_u, m + 1)
                v.tensor_tensor(CBS[j % 2][0:h, :], PU[0:h, :], CBS[j % 2][0:h, :], ALU.mult).then_inc(s_w, 1)

            def tail_b(n, g, final):
                dve.wait_ge(s_down, n * FT + FT)
                for b in range(2):
                    xv = X[:, bass.ds(g.x + 2 * b, 2), :]
                    last = v.tensor_tensor(xv, PY[b][:, :].rearrange("p (t d) -> p t d", t=2), xv, ALU.add)
                    if b == 1:
                        last.then_inc(s_yr, 1)
                if final:
                    settle()
                    v.sem_inc(s_out, 1)

            def proj(g, c, hb, us):
                q = g.at * GT + c
                u = us["proj"]
                ready(u, hb)
                dve.wait_ge(s_ro, q + 1)
                t = T[u % 2][:, :].rearrange("p (h a d) -> p h a d", a=2, d=8)
                tb = rope[:, g.at * GT + c, :]
                rc = RC[:, :].rearrange("p (h a d) -> p h a d", a=2, d=8)
                rt = RT[:, :].rearrange("p (h a d) -> p h a d", a=2, d=8)
                cos = bc(bc(tb[:, 0:8], 1, 2), 1, 2 * HEADS)
                v.tensor_tensor(rc, t, cos, ALU.mult)
                sin = bc(tb[:, 8:16], 1, 2 * HEADS)
                v.scalar_tensor_tensor(rt[:, :, 0, :], t[:, :, 1, :], -1.0, sin, ALU.mult, ALU.mult)
                v.tensor_tensor(rt[:, :, 1, :], t[:, :, 0, :], sin, ALU.mult).then_inc(s_rt, 1)
                dve.wait_ge(s_rt, q + 1)
                v.sem_inc(s_tf[u % 2], 1)

            def phi(g, c, hb, us):
                q = g.at * GT + c
                dve.wait_ge(s_ro, q + 2)
                v.tensor_scalar(RT[:, :], RC[:, :], 0.0, None, ALU.min).then_inc(s_mn, 1)
                dve.wait_ge(s_ex, q + 1)
                v.scalar_tensor_tensor(RC[:, :], RC[:, :], 0.0, RT[:, :], ALU.max, ALU.add)
                settle()
                if c == 0:
                    dve.wait_ge(s_dec, g.at + 1)
                dve.wait_ge(s_av, q * 4 + 4)
                v.tensor_tensor(QK[c % 2][:, :].rearrange("p (h d) -> p h d", d=DH),
                                RC[:, :].rearrange("p (h d) -> p h d", d=DH),
                                bc(DEC[:, c, :], 2, DH), ALU.mult).then_inc(s_qk, 1)

            def masked(q, b, n, hb):
                ready(n, hb)
                dve.wait_ge(s_av, q * 4 + b + 7)
                v.tensor_tensor(AM[b % 2][:, :, :], T[n % 2][:, :].rearrange("p (h t) -> p h t", h=4),
                                bc(CN[:, C_CAUSAL:C_CAUSAL + P], 1, 4), ALU.mult).then_inc(s_tf[n % 2], 1)

            def core(g, c, hb, us):
                q = g.at * GT + c
                n = us["core"]
                ready(n, hb)
                v.tensor_tensor(DS[:, :, :], T[n % 2][:, 0:16 * VW].rearrange("p (a n) -> p a n", a=2), block2,
                                ALU.mult).then_inc(s_tf[n % 2], 1)
                masked(q, 0, n + 1, hb)

            def core_1(g, c, hb, us):
                masked(g.at * GT + c, 1, us["core_1"], hb)
                v.tensor_tensor(DS[:, :, :], S[:, :, :], DS[:, :, :], ALU.add)

            def core_2(g, c, hb, us):
                q = g.at * GT + c
                masked(q, 2, us["core_2"], hb)
                settle()
                dve.wait_ge(s_inter, q + 1)
                for a in range(2):
                    last = v.tensor_scalar(S[:, a, :], DS[:, a, :], PT[:, a, c:c + 1], None, ALU.mult)
                last.then_inc(s_st, 1)

            def core_3(g, c, hb, us):
                masked(g.at * GT + c, 3, us["core_3"], hb)

            def attend(g, c, hb, us):
                q = g.at * GT + c
                dve.wait_ge(s_av, q * 4 + 12)
                o = T2[:, 0:HEADS * VW].rearrange("p (h d) -> p h d", d=VW)
                v.tensor_scalar(DN[:, :], o[:, :, DH], DEN_EPS, None, ALU.add)
                settle()
                v.reciprocal(RD[:, :], DN[:, :])
                settle()
                v.tensor_tensor(Y[:, :, :], o[:, :, 0:DH], bc(RD[:, :], 2, DH), ALU.mult).then_inc(s_or, 1)

            def wo_turn(g, c, hb, us):
                q = g.at * GT + c
                n = us["wo_turn"]
                dve.wait_ge(s_yhi, q + 1)
                v.tensor_tensor(YT[1][:, :, :], T[n % 2][:, 0:D].rearrange("p (k t) -> p k t", k=KD),
                                YT[0][:, :, :].bitcast(F32), ALU.subtract).then_inc(s_tf[n % 2], 1)

            def wo(g, c, hb, us):
                n = us["wo"]
                dve.wait_ge(s_boa, g.at + 1)
                ready(n, hb)
                xv = X[:, g.x + c, :]
                v.tensor_tensor(xv, T[n % 2][:, 0:D], xv, ALU.add).then_inc(s_tf[n % 2], 1)

            v.sem_inc(s_st, 1)
            v.sem_inc(s_or, 1)
            run(dve, {"split": split, "norm_stats": norm_stats, "norm_var": norm_var, "norm_scale": norm_scale,
                      "norm_turn": norm_turn, "norm_first": norm_first, "norm_mid": norm_mid, "norm_last": norm_last, "ffn": ffn, "tail_b": tail_b,
                      "proj": proj, "phi": phi, "core": core, "core_1": core_1, "core_2": core_2, "core_3": core_3,
                      "attend": attend, "wo_turn": wo_turn, "wo": wo})

        @block.tensor
        def _(pe):
            mm = nc.tensor.matmul
            PASSES = ((0, 0), (0, 1), (1, 0))

            def fresh(u, hb):
                need(pe, s_tf[u % 2], hb + u // 2)

            def taken(u, hb):
                pe.wait_ge(s_tf[u % 2], hb + u // 2 + 1)

            def norm_turn(norm, hb, us):
                pe.wait_ge(s_xn, norm.r + 1)
                for k in range(KD):
                    u = us["norm_turn"] + k
                    fresh(u, hb)
                    for c in range(GT):
                        last = nc.tensor.transpose(T[u % 2][:, c * P:(c + 1) * P], XN[:, c, k * P:(k + 1) * P], ident)
                    last.then_inc(s_tr[u % 2], 1)

            def norm_first(norm, hb, us):
                kind = norm.kind
                u = us["norm_first"]
                taken(us["norm_turn"] + (us["norm_turn"] + u + 1) % 2, hb)
                fresh(u, hb)
                if kind == "A":
                    n = 0
                    for k in range(KD):
                        for a, b in PASSES:
                            last = mm(T[u % 2][0:HEADS, :], WP[b][:, k, 3 * D:QKV], XT[norm.buf][a][:, k, :],
                                      start=n == 0, stop=n == 3 * KD - 1)
                            n += 1
                else:
                    for c in range(GT):
                        at = c * 2 * NR
                        for k in range(KD):
                            for a in range(2):
                                w = (2 - a) * NR
                                last = mm(T[u % 2][:, at:at + w], XT[norm.buf][a][:, k, c * P:(c + 1) * P], WR[:, k, 0:w],
                                          start=k == 0 and a == 0, stop=k == KD - 1 and a == 1, skip_group_check=True)
                last.then_inc(s_tr[u % 2], 1)

            def norm_last(norm, hb, us):
                u = us["norm_last"]
                fresh(u, hb)
                if norm.kind == "A":
                    pe.wait_ge(s_dp, norm.g.at + 1)
                    ends = DP[:, :].rearrange("h (c t) -> h c t", c=GT)[:, :, P - 1]
                    for a in range(2):
                        mm(T[u % 2][:, P + a * GT:P + (a + 1) * GT], expand[:, a, :], ends, start=True, stop=True)
                    for c in range(GT):
                        last = nc.tensor.transpose(T[u % 2][:, c * HEADS:(c + 1) * HEADS], DP[:, c * P:(c + 1) * P],
                                                   CN[0:HEADS, C_ID:C_ID + HEADS])
                else:
                    pe.wait_ge(s_comb, norm.f + 1)
                    for c in range(GT):
                        last = nc.tensor.transpose(T[u % 2][0:2 * NR, c * P:(c + 1) * P], CHL[:, c, :], ident)
                last.then_inc(s_tr[u % 2], 1)

            def down(n, j):
                h = HID - j * P if j == FT - 1 else P
                m = n * FT + j
                pe.wait_ge(s_hl, m + 1)
                if j == 0:
                    need(pe, s_yr, n)
                for t in range(GT):
                    for i, (a, b) in enumerate(PASSES):
                        last = mm(PY[t // 2][:, (t % 2) * D:(t % 2 + 1) * D], (HH, HL)[a][j % 2][0:h, t * P:(t + 1) * P],
                                  WD[b][0:h, j, :], start=(j == 0 and i == 0 and t % 2 == 0),
                                  stop=(j == FT - 1 and i == 2), skip_group_check=True)
                last.then_inc(s_down, 1)

            def ffn(buf, n, j):
                h = HID - j * P if j == FT - 1 else P
                m = n * FT + j
                col = slice(j * P, j * P + h)
                if isinstance(n, int) and n == 0 and j in PART_AT:
                    p = PART_AT.index(j)
                    pe.wait_ge(s_lo, sum(splits[:sum(batch[:p + 2])]))
                def spread():
                    need(pe, s_cbs, m)
                    mm(PC[0:h, :], SEL[:, col], CT[buf][:, :], start=True, stop=True).then_inc(s_cb, 1)

                if j > 0:
                    spread()
                for w, out, free, ready in ((WG, PG, s_s, s_g), (WU, PU, s_w, s_u)):
                    need(pe, free, m)
                    i = 0
                    for k in range(KD):
                        for a, b in PASSES:
                            last = mm(out[0:h, :], w[b][:, k, col], XT[buf][a][:, k, :], start=i == 0, stop=i == 3 * KD - 1)
                            i += 1
                    last.then_inc(ready, 1)
                if j == 0:
                    pe.wait_ge(s_ct, n + 1)
                    spread()

            def proj(g, c, hb, us):
                for u, n0, n1 in ((us["proj"], 0, 2 * D), (us["proj"] + 1, 2 * D, 3 * D)):
                    fresh(u, hb)
                    i = 0
                    for k in range(KD):
                        for a, b in PASSES:
                            last = mm(T[u % 2][:, 0:n1 - n0], XT["A"][a][:, k, c * P:(c + 1) * P], WP[b][:, k, n0:n1],
                                      start=i == 0, stop=i == 3 * KD - 1)
                            i += 1
                    last.then_inc(s_tr[u % 2], 1)

            def turn(g, c, hb, us):
                u = us["turn"]
                pe.wait_ge(s_qk, g.at * GT + c + 1)
                fresh(u, hb)
                for b in range(4):
                    last = nc.tensor.transpose(T[u % 2][:, b * P:(b + 1) * P], QK[c % 2][:, b * P:(b + 1) * P], ident)
                last.then_inc(s_tr[u % 2], 1)

            def scores(b, u, hb):
                fresh(u, hb)
                row = 32 * b
                for i in range(4):
                    last = mm(T[u % 2][:, i * P:(i + 1) * P], KT[i % 2][row:row + 32, i // 2, :],
                              QT[row:row + 32, i // 2, :], start=True, stop=True)
                last.then_inc(s_tr[u % 2], 1)

            def values(c, b, u, hb):
                taken(u, hb)
                for i in range(4):
                    hd = 8 * (i // 2) + 2 * b + i % 2
                    last = mm(T2[:, hd * VW:(hd + 1) * VW], AM[b % 2][:, i, :], VA[c % 2][:, hd, :], start=False,
                              stop=hd == HEADS - 1, skip_group_check=True)
                last.then_inc(s_av, 1)

            def core(g, c, hb, us):
                q = g.at * GT + c
                taken(us["turn"], hb)
                pe.wait_ge(s_st, q + 1)
                pe.wait_ge(s_or, q + 1)
                for a in range(2):
                    last = mm(T2[:, a * 8 * VW:(a + 1) * 8 * VW], QT[:, a, :], S[:, a, :], start=a == 0, stop=False,
                              skip_group_check=True)
                last.then_inc(s_inter, 1)
                u = us["core"]
                fresh(u, hb)
                for a in range(2):
                    last = mm(T[u % 2][:, a * 8 * VW:(a + 1) * 8 * VW], QK[c % 2][:, D + a * P:D + (a + 1) * P],
                              VA[c % 2][:, 8 * a:8 * a + 8, :], start=True, stop=True)
                last.then_inc(s_tr[u % 2], 1)
                scores(0, u + 1, hb)

            def core_1(g, c, hb, us):
                values(c, 0, us["core"] + 1, hb)
                scores(1, us["core_1"], hb)

            def core_2(g, c, hb, us):
                values(c, 1, us["core_1"], hb)
                scores(2, us["core_2"], hb)

            def core_3(g, c, hb, us):
                values(c, 2, us["core_2"], hb)
                scores(3, us["core_3"], hb)

            def core_4(g, c, hb, us):
                values(c, 3, us["core_3"], hb)

            def wo_turn(g, c, hb, us):
                u = us["wo_turn"]
                pe.wait_ge(s_or, g.at * GT + c + 2)
                fresh(u, hb)
                yv = Y[:, :, :].rearrange("p h d -> p (h d)")
                for k in range(KD):
                    last = nc.tensor.transpose(T[u % 2][:, k * P:(k + 1) * P], yv[:, k * P:(k + 1) * P], ident)
                last.then_inc(s_tr[u % 2], 1)

            def wo(g, c, hb, us):
                u = us["wo"]
                if (us["wo_turn"] - u) % 2:
                    taken(us["wo_turn"], hb)
                fresh(u, hb)
                i = 0
                for k in range(KD):
                    for a, b in PASSES:
                        last = mm(T[u % 2][:, 0:D], YT[a][:, k, :], WO[b][:, k, :], start=i == 0, stop=i == 3 * KD - 1)
                        i += 1
                last.then_inc(s_tr[u % 2], 1)

            def tail_a(n):
                down(n, FT - 2)

            def tail_b(n, g, final):
                down(n, FT - 1)

            pe.sem_inc(s_av, 8)
            pe.wait_ge(s_const, 16)
            pe.wait_ge(s_wready, 1)
            run(pe, {"norm_turn": norm_turn, "norm_first": norm_first, "norm_last": norm_last, "ffn": ffn, "tail_a": tail_a,
                     "tail_b": tail_b, "down": down, "proj": proj, "turn": turn, "core": core, "core_1": core_1, "core_2": core_2,
                     "core_3": core_3, "core_4": core_4, "wo_turn": wo_turn, "wo": wo})


_INS = ["L0_attn_x", "L0_attn_Wq", "L0_attn_Wk", "L0_attn_Wv", "L0_attn_Wg", "L0_attn_bg", "L0_attn_Wo", "L0_attn_bo",
        "L0_ffn_gate_w", "L0_ffn_w_gate", "L0_ffn_w_up", "L0_ffn_w_down", "L0_ffn_shgate_w", "L0_ffn_shw_gate",
        "L0_ffn_shw_up", "L0_ffn_shw_down"]


def kernel(**inputs):
    import concourse.bacc as _bacc
    from concourse.bass_utils import run_bass_kernel_spmd as _run

    nc = _bacc.Bacc("TRN2", target_bir_lowering=False, num_devices=1)
    arrays, args = {}, []
    for name in _INS:
        a = np.ascontiguousarray(inputs[name])
        arrays[f"in_{name}"] = a
        args.append(nc.dram_tensor(f"in_{name}", a.shape, mybir.dt.from_np(a.dtype), kind="ExternalInput").ap())
    c = constants()
    arrays["in_constants"] = c
    args.append(nc.dram_tensor("in_constants", c.shape, F32, kind="ExternalInput").ap())
    c = selector()
    arrays["in_selector"] = c
    args.append(nc.dram_tensor("in_selector", c.shape, F32, kind="ExternalInput").ap())
    args.append(nc.dram_tensor("out", (B, L, D), F32, kind="ExternalOutput").ap())
    build(nc, *args)
    r = _run(nc, [arrays], core_ids=[0])
    return r.results[0]["out"]
```

```python
import concourse.bass as bass
from concourse import mybir
from collections import namedtuple
from contextlib import ExitStack
import numpy as np

F32 = mybir.dt.float32
F32R = mybir.dt.float32r
U32 = mybir.dt.uint32
ALU = mybir.AluOpType
ACT = mybir.ActivationFunctionType
AX = mybir.AxisListType

B, L, D = 4, 1024, 256
HEADS, DH = 16, 16
E, HE, HS = 8, 176, 352
P = 128
KD = D // P
GT = 4
GN = GT * P
NT = B * L // P
NG = NT // GT
XR = 4
STAGE = 7 * D
HID = E * HE + HS
FT = -(-HID // P)
HE_ALL = E * HE
NR = E + 2
VW = DH + 2
QKV = 3 * D + HEADS
LN_EPS, DEN_EPS = 1e-5, 1e-6
BETA_MIN, BETA_MAX = 0.8, 0.9995

C_ID = 0
C_IOTA = C_ID + P
C_HALF = C_IOTA + E
C_FIRST = C_HALF + GT
C_CAUSAL = C_FIRST
C_BLOCK = C_CAUSAL + P
C_ROPE = C_BLOCK + 8 * VW
C_PAR = C_ROPE + NT * 16
C_KEEP = C_PAR + 2
C_EXP = C_KEEP + NT
C_ALL = C_EXP + 2 * P

PARTS = ((0, 3), (3, 6), (6, E))
PART_AT = tuple(a * HE // P for a, _ in PARTS)


def constants():
    c = np.zeros((P, C_ALL), np.float32)
    p = np.arange(P)
    c[:, C_ID:C_ID + P] = np.eye(P)
    c[:, C_CAUSAL:C_CAUSAL + P] = p[:, None] <= p[None, :]
    c[:, C_BLOCK:C_BLOCK + 8 * VW] = (p[:, None] // DH) == (np.arange(8 * VW)[None, :] // VW)
    half = DH // 2
    inv = (np.float32(1.0) / np.float32(10000.0) ** (np.arange(half, dtype=np.float32) / np.float32(half))).astype(np.float32)
    ang = (np.arange(L, dtype=np.float32)[:, None] * inv[None, :]).astype(np.float32)
    tab = np.concatenate([np.cos(ang), np.sin(ang)], 1).astype(np.float32)
    tab = tab.reshape(L // P, P, 16).transpose(1, 0, 2)
    c[:, C_ROPE:C_ROPE + NT * 16] = np.tile(tab, (1, B, 1)).reshape(P, NT * 16)
    c[:, C_PAR] = (p // DH) % 2 == 0
    c[:, C_PAR + 1] = (p // DH) % 2 == 1
    c[:, C_IOTA:C_IOTA + E] = np.arange(E)
    c[:, C_KEEP:C_KEEP + NT] = (np.arange(NT) % (L // P)) != L // P - 1
    for h in range(HEADS):
        c[h, C_EXP + h * DH:C_EXP + (h + 1) * DH] = 1.0
    c[:, C_HALF:C_HALF + GT] = -0.5
    return c


def load_parts(j):
    lo, hi = j * P, min(j * P + P, HID)
    cut = [(a, b, e) for e, a, b in ((e, max(lo, e * HE), min(hi, (e + 1) * HE if e < E else HID)) for e in range(E + 1)) if a < b]
    if len(cut) == 1:
        a, b, e = cut[0]
        cut = [(a, (a + b) // 2, e), ((a + b) // 2, b, e)]
    return [(a - lo, b - lo, e) for a, b, e in cut]


def ring(buf, j):
    return (j + FT * buf) % 4


def ring_loads(n, buf, j):
    return 2 * 16 * FT // 4 * (n - buf) + 32 * ((FT * buf + j) // 4 + 1)


Group = namedtuple("Group", "at x")


def group(g):
    return Group(g, g % XR * GT)


def need(eng, sem, value):
    if not isinstance(value, int) or value > 0:
        eng.wait_ge(sem, value)


def bc(ap, axis, n):
    v = ap.unsqueeze(axis)
    s = list(v.shape)
    s[axis] = n
    return v.broadcast_to(s)


USES = {"proj": 2, "turn": 1, "core": 2, "core_1": 1, "core_2": 1, "core_3": 1, "wo_turn": 1, "wo": 1,
        "norm_turn": 2, "norm_first": 1, "norm_last": 1}
U_FIRST = 2 * 4
U_SECOND = 2 * 4 + 2 * 10
U_LOOP = 3 * 4 + GT * 10

NORM = (("norm_stats", 0), ("norm_var", 1), ("norm_scale", 1), ("norm_turn", 2), ("norm_first", 1), ("norm_mid", 2), ("norm_last", 2))
CHUNK = (("proj", 0), ("phi", 1), ("turn", 2), ("core", 1), ("core_1", 1), ("core_2", 1), ("core_3", 1), ("core_4", 1),
         ("attend", 0), ("wo_turn", 1), ("wo", 1))
Norm = namedtuple("Norm", "kind buf r g f prev")


WO = sum(gap for _, gap in CHUNK)


def slots(norms, chunks):
    out = {}
    for at, norm in norms:
        for step, gap in NORM:
            at += gap
            out.setdefault(at, []).append([step, norm])
    for at, g, c in chunks:
        for step, gap in CHUNK:
            at += gap
            out.setdefault(at, []).append([step, g, c])
    for steps in out.values():
        steps.sort(key=lambda s: s[0] in ("norm_stats", "norm_var", "norm_scale"))
    return out


def ordered(hb, table, tiles, tails):
    k = 0
    own = {}
    for half in range(max([*table, *[2 * t + 1 for t in [*tiles, *tails]]]) + 1):
        slot = half // 2
        if half % 2 == 0 and slot in tiles:
            if tiles[slot][2] == 0:
                yield ("spread", *tiles[slot][:2])
            yield ("ffn", *tiles[slot])
        if half % 2:
            yield from tails.get(slot, ())
            if slot in tiles and tiles[slot][2] >= 2:
                yield ("down", tiles[slot][1], tiles[slot][2] - 2)
        for step, who, *c in table.get(half, ()):
            mine = own.setdefault((id(who), *c), {})
            if step in USES:
                mine[step] = k
                k += USES[step]
            yield (step, who, *c, hb, dict(mine))


def tiles_at(slot, buf, n):
    return {slot + j: (buf, n, j) for j in range(FT)}


def tails_at(slot, n, g, final):
    return {slot: [("tail_a", n)], slot + 1: [("tail_b", n, g, final)]}


CH = 6


def first():
    norm = Norm("F1", 0, 0, group(0), 0, None)
    for s in ordered(0, slots([(0, norm)], []), {}, {}):
        yield s
        if s[0] == "norm_scale":
            yield ("routers",)
        if s[0] == "norm_turn":
            yield ("split", 0)
            yield ("split", 1)
    yield ("split", 2)
    splits = {slot: [("split", 3 + k)] for k, slot in enumerate((0, 1, 2, 3, 5, 6, 7, 8))}
    yield from ordered(2, slots([(13, Norm("F1", 1, 1, group(1), 1, None))], []), tiles_at(0, 0, 0), splits)


def second():
    a0, f2 = Norm("A", "A", 2, group(0), None, 0), Norm("F1", 0, 3, group(2), 2, 0)
    yield from ordered(U_FIRST // 2, slots([(3, a0), (15, f2)], [(11 + CH * c, group(0), c) for c in range(2)]),
                       tiles_at(0, 1, 1), tails_at(0, 0, group(0), False))


def loop_base(i):
    return (i - 2) * (U_LOOP // 2) + (U_FIRST + U_SECOND) // 2


def middle(i, back3, back2, back1, this, ahead):
    norms = [(CH, Norm("A", "A", 3 * i - 2, back1, None, i - 1)),
             (CH + WO, Norm("F2", 1, 3 * i - 1, back2, 2 * i - 1, 2 * i - 3)),
             (32, Norm("F1", 0, 3 * i, ahead, 2 * i, 2 * i - 2))]
    chunks = [(0, back2, 2), (CH, back2, 3), (28, back1, 0), (42, back1, 1)]
    tiles = tiles_at(0, 0, 2 * i - 2) | tiles_at(FT, 1, 2 * i - 1)
    tails = tails_at(0, 2 * i - 3, back1 if back3 is None else back3, back3 is not None) | tails_at(FT, 2 * i - 2, this, False)
    yield from ordered(loop_base(i), slots(norms, chunks), tiles, tails)


def last():
    i = NG - 1
    g3, g2, g1, g0 = (group(i - k) for k in (3, 2, 1, 0))
    c1 = 2 * CH + 2
    c0 = c1 + 4 * CH + 2
    t1, t0 = 2 * FT, 3 * FT + 1
    norms = [(c1 - 8, Norm("A", "A", 3 * i - 2, g1, None, i - 1)),
             (CH + WO, Norm("F2", 1, 3 * i - 1, g2, 2 * i - 1, 2 * i - 3)),
             (c0 - 8, Norm("A", "A", 3 * i, g0, None, i)),
             (c1 + 3 * CH + WO, Norm("F2", 0, 3 * i + 1, g1, 2 * i, 2 * i - 2)),
             (c0 + 3 * CH + WO, Norm("F2", 1, 3 * i + 2, g0, 2 * i + 1, 2 * i - 1))]
    chunks = [(0, g2, 2), (CH, g2, 3)] + [(at + CH * c, g, c) for at, g in ((c1, g1), (c0, g0)) for c in range(GT)]
    tiles = tiles_at(0, 0, 2 * i - 2) | tiles_at(FT, 1, 2 * i - 1) | tiles_at(t1, 0, 2 * i) | tiles_at(t0, 1, 2 * i + 1)
    tails = (tails_at(0, 2 * i - 3, g3, True) | tails_at(FT, 2 * i - 2, g0, False) | tails_at(2 * FT, 2 * i - 1, g2, True)
             | tails_at(t1 + FT, 2 * i, g1, True) | tails_at(t0 + FT, 2 * i + 1, g0, True))
    yield from ordered(loop_base(i), slots(norms, chunks), tiles, tails)


def run(eng, parts):
    def do(step, *a):
        if step in parts:
            parts[step](*a)

    for s in [*first(), *second(), *middle(2, None, *(group(g) for g in range(4)))]:
        do(*s)
    with eng.Fori(3, NG - 1) as i:
        gs = [Group(i + k, eng.snap((i + k) % XR * GT)) for k in (-3, -2, -1, 0, 1)]
        for s in middle(i, *gs):
            do(*s)
    for s in last():
        do(*s)


def build(nc, x_d, wq_d, wk_d, wv_d, wg_d, bg_d, wo_d, bo_d, gw_d, eg_d, eu_d, ed_d, sgw_d, sg_d, su_d, sd_d, c_d, comb_d, out_d):
    ctx = ExitStack()
    with ctx:
        def sb(name, shape, dt=F32):
            return ctx.enter_context(nc.sbuf_tensor(name, shape, dt))

        def pb(name):
            return ctx.enter_context(nc.psum_tensor(name, [P, 512], F32))

        def sem(name):
            return ctx.enter_context(nc.semaphore(name))

        X = sb("X", [P, XR * GT, D])
        CN = sb("CN", [P, C_ALL])
        WG = [sb(f"WG{k}", [P, KD, HID], F32R) for k in "hl"]
        WU = [sb(f"WU{k}", [P, KD, HID], F32R) for k in "hl"]
        WD = [sb(f"WD{k}", [P, FT, D], F32R) for k in "hl"]
        WP = [sb(f"WP{k}", [P, KD, QKV], F32R) for k in "hl"]
        WO = [sb(f"WO{k}", [P, KD, D], F32R) for k in "hl"]
        R32 = sb("R32", [P, KD, NR])
        WR = sb("WR", [P, KD, 2 * NR], F32R)
        BO = sb("BO", [P, D])
        HBG = sb("HBG", [HEADS, 1])
        ST = sb("ST", [P, GT, 6])
        MV = sb("MV", [P, GT, 2])
        XN = sb("XN", [P, GT, D])
        VE = sb("VE", [P, GT])
        RS = sb("RS", [P, GT])
        XT = {k: [sb(f"XT{k}{h}", [P, KD, GN], F32R) for h in "hl"] for k in (0, 1, "A")}
        LG = sb("LG", [P, GT, NR])
        TOP = sb("TOP", [P, GT, 8])
        IDX = sb("IDX", [P, GT, 8], U32)
        IDF = sb("IDF", [P, GT, 2])
        GAP = sb("GAP", [P, GT])
        E2 = sb("E2", [P, GT])
        SGT = sb("SGT", [P, GT])
        DEN2 = sb("DEN2", [P, GT])
        W12 = sb("W12", [P, 2, GT])
        HOT = sb("HOT", [P, 2, GT, E])
        CMB = sb("CMB", [P, GT, NR])
        CT = sb("CT", [NR, GN])
        CBS = [sb(f"CBS{k}", [P, GN]) for k in range(4)]
        TH = [sb(f"TH{k}", [P, GN]) for k in range(2)]
        HH = [sb(f"HH{k}", [P, GN], F32R) for k in range(2)]
        HL = [sb(f"HL{k}", [P, GN], F32R) for k in range(2)]
        BT = sb("BT", [HEADS, GN])
        ZR = sb("ZR", [HEADS, P])
        DP = sb("DP", [HEADS, GN])
        DEC = sb("DEC", [P, GT, 2 * HEADS])
        PT = sb("PT", [P, 2, GT])
        SCRATCH = sb("SCRATCH", [P, 2 * STAGE])
        STG = [SCRATCH[:, k * STAGE:(k + 1) * STAGE] for k in range(2)]
        RC, RT, QK0, QK1 = (SCRATCH[:, k * 2 * D:(k + 1) * 2 * D] for k in range(4))
        QK = [QK0, QK1]
        AM0, AM1 = (SCRATCH[:, k * D:(k + 2) * D].rearrange("p (h t) -> p h t", h=4) for k in (11, 8))
        VA = [sb(f"VA{k}", [P, HEADS, VW]) for k in range(2)]
        QT = SCRATCH[:, 10 * D:11 * D].rearrange("p (a t) -> p a t", a=2)
        KT = [sb(f"KT{k}", [P, 2, P], F32R) for k in "hl"]
        QM = [sb(f"QM{k}", [P, 2, 2, P], F32R) for k in "hl"]
        AM = [AM0, AM1]
        S = sb("S", [P, 2, 8 * VW])
        DS = sb("DS", [P, 2, 8 * VW])
        DN = sb("DN", [P, HEADS])
        RD = sb("RD", [P, HEADS])
        Y = sb("Y", [P, HEADS, DH])
        YT = [sb(f"YT{k}", [P, KD, P], F32R) for k in "hl"]

        T = [pb(f"T{k}") for k in range(2)]
        T2 = pb("T2")
        PG, PU = [pb(f"PG{k}") for k in range(2)], pb("PU")
        PY = [pb(f"PY{k}") for k in range(2)]

        ident = CN[:, C_ID:C_ID + P]
        rope = CN[:, C_ROPE:C_ROPE + NT * 16].rearrange("p (t c) -> p t c", c=16)
        expand = CN[0:HEADS, C_EXP:C_EXP + 2 * P].rearrange("p (a c) -> p a c", a=2)
        block2 = bc(CN[:, C_BLOCK:C_BLOCK + 8 * VW], 1, 2)

        s_tables = sem("tables_loaded")
        s_const, s_x0, s_x1, s_xrest, s_small, s_bo = (sem(n) for n in (
            "const_loaded", "x0_loaded", "x1_loaded", "xrest_loaded", "router_loaded", "bo_loaded"))
        s_stage = [sem(f"stage{k}_loaded") for k in range(2)]
        s_hi, s_lo, s_prep, s_wready = sem("weight_high"), sem("weight_low"), sem("prepared"), sem("weights_ready")
        s_tr = [sem(f"tmp{k}_ready") for k in range(2)]
        s_tf = [sem(f"tmp{k}_free") for k in range(2)]
        s_var, s_rstd, s_xn, s_xh = sem("var"), sem("rstd"), sem("xn"), sem("xt_high")
        s_gap, s_e2, s_comb, s_spread = sem("gap"), sem("top2_exp"), sem("comb"), sem("comb_stored")
        s_cl = [sem(f"comb{k}_loaded") for k in range(4)]
        s_g, s_th, s_u, s_w, s_s = (sem(n) for n in (
            "gate", "gate_tanh", "up", "up_weighted", "gate_silu"))
        s_h, s_hh, s_hl, s_down, s_yr = (sem(n) for n in (
            "hidden", "hidden_high", "hidden_low", "down", "y_added"))
        s_dp, s_dec, s_boa = sem("decay"), sem("decay_turned"), sem("bo_added")
        s_rt, s_ro, s_mn, s_ex, s_qk = (sem(n) for n in (
            "rope_parts", "rope_sum", "phi_min", "phi_exp", "qk_scaled"))
        s_qh = sem("qk_turned_high")
        s_inter, s_or, s_st = (sem(n) for n in ("inter", "core_read", "state"))
        s_av, s_yhi, s_out, s_store = sem("scores_used"), sem("attn_y_high"), sem("out_ready"), sem("stored")

        xt_view = x_d.rearrange("b (t p) d -> p (b t) d", p=P)
        ot_view = out_d.rearrange("b (t p) d -> p (b t) d", p=P)
        block = ctx.enter_context(nc.Block())

        def kcols(w, k):
            return w[k * P:(k + 1) * P, :]

        def hidden_piece(w, s, dst, a, b):
            n = (b - a) * HE
            full = n + (HS if b == E else 0)
            ld = []
            for k in range(KD):
                ld.append(((P, k * full, k * full + n, b - a), w[a:b, k * P:(k + 1) * P, :].rearrange("e p h -> p e h")))
                if b == E:
                    ld.append(((P, k * full + n, (k + 1) * full, 0), kcols(s, k)))
            return ld, [(P, 0, KD * full, dst[0][:, :, a * HE:a * HE + full], dst[1][:, :, a * HE:a * HE + full])]

        edf = ed_d.rearrange("e h d -> (e h) d")

        def down_piece(t0, t1):
            if t1 * P <= HE_ALL:
                return ([((P, 0, (t1 - t0) * D, t1 - t0), edf[t0 * P:t1 * P, :].rearrange("(t p) d -> p t d", p=P))],
                        [(P, 0, (t1 - t0) * D, WD[0][:, t0:t1, :], WD[1][:, t0:t1, :])])
            ne, ns = HE_ALL // P - t0, HS // P
            rest = HS - ns * P
            m = ne + ns
            return ([((P, 0, ne * D, ne), edf[t0 * P:HE_ALL, :].rearrange("(t p) d -> p t d", p=P)),
                     ((P, ne * D, m * D, ns), sd_d[0:ns * P, :].rearrange("(t p) d -> p t d", p=P)),
                     ((rest, m * D, (m + 1) * D, 0), sd_d[ns * P:HS, :])],
                    [(P, 0, m * D, WD[0][:, t0:t0 + m, :], WD[1][:, t0:t0 + m, :]),
                     (rest, m * D, (m + 1) * D, WD[0][0:rest, t0 + m, :], WD[1][0:rest, t0 + m, :])])

        pieces = []
        for n, (a, b) in enumerate(PARTS):
            pieces += [hidden_piece(eg_d, sg_d, WG, a, b), hidden_piece(eu_d, su_d, WU, a, b),
                       down_piece(PART_AT[n], PART_AT[n + 1] if b < E else FT)]
        loads = [((P, k * QKV + w * D, k * QKV + w * D + m.shape[1], 0), kcols(m, k))
                 for w, m in enumerate((wq_d, wk_d, wv_d, wg_d)) for k in range(KD)]
        pieces.append((loads, [(P, 0, KD * QKV, WP[0][:, :, :], WP[1][:, :, :])]))
        pieces.append(([((P, 0, KD * D, KD), wo_d.rearrange("(k p) n -> p k n", p=P))],
                       [(P, 0, KD * D, WO[0][:, :, :], WO[1][:, :, :])]))
        staged = [0, 0]
        arrive = []
        for k, (ld, _) in enumerate(pieces):
            staged[k % 2] += 16 * len(ld)
            arrive.append(staged[k % 2])
        splits = [len(c) for _, c in pieces]

        def split_by(k):
            return sum(splits[:k + 1])

        def shaped(ap, like):
            if len(like.shape) == 2:
                return ap
            return ap.rearrange("p (a b) -> p a b", a=like.shape[1])

        @block.sync
        def _(sp):
            sp.dma_start(X[:, 0:GT, :], xt_view[:, 0:GT, :]).then_inc(s_x0, 16)
            sp.dma_start(CN[:, 0:C_FIRST], c_d[:, 0:C_FIRST]).then_inc(s_const, 16)
            for k, (ld, _) in enumerate(pieces):
                if k >= 2:
                    sp.wait_ge(s_lo, split_by(k - 2))
                for (rows, a, b, t), src in ld:
                    dst = STG[k % 2][0:rows, a:b]
                    if t:
                        dst = dst.rearrange("p (t n) -> p t n", t=t)
                    sp.dma_start(dst, src).then_inc(s_stage[k % 2], 16)
                if k == 3:
                    sp.dma_start(CN[:, C_FIRST:C_ALL], c_d[:, C_FIRST:C_ALL]).then_inc(s_tables, 16)
                if k == 5:
                    sp.dma_start(X[:, GT:2 * GT, :], xt_view[:, GT:2 * GT, :]).then_inc(s_x1, 16)
            sp.dma_start(BO[:, :], bo_d.rearrange("(a n) -> a n", a=1).broadcast_to([P, D])).then_inc(s_bo, 16)
            sp.dma_start(X[:, 2 * GT:3 * GT, :], xt_view[:, 2 * GT:3 * GT, :]).then_inc(s_xrest, 16)
            sp.wait_ge(s_xrest, 16)
            sp.dma_start(X[:, 3 * GT:4 * GT, :], xt_view[:, 3 * GT:4 * GT, :]).then_inc(s_xrest, 16)
            for g in range(NG):
                at = g % XR * GT
                sp.wait_ge(s_out, g + 1)
                sp.dma_start(ot_view[:, g * GT:(g + 1) * GT, :], X[:, at:at + GT, :]).then_inc(s_store, 16)
                if g + XR < NG:
                    sp.wait_ge(s_store, 16 * g + 16)
                    sp.wait_ge(s_xrest, 16 * g + 32)
                    sp.dma_start(X[:, at:at + GT, :], xt_view[:, (g + XR) * GT:(g + XR + 1) * GT, :]).then_inc(s_xrest, 16)
            sp.wait_ge(s_store, 16 * NG)

        @block.gpsimd
        def _(pool):
            pool.wait_ge(s_prep, 1)
            with nc.allow_non_contiguous_dma("router columns"):
                for k in range(KD):
                    pool.dma_start(R32[:, k, 0:E], gw_d[:, k * P:(k + 1) * P].rearrange("e p -> p e")).then_inc(s_small, 16)
                    pool.dma_start(R32[:, k, E:E + 1], sgw_d[k * P:(k + 1) * P].rearrange("(p a) -> p a", a=1)).then_inc(s_small, 16)
                pool.dma_start(HBG[:, :], bg_d.rearrange("(p a) -> p a", a=1)).then_inc(s_small, 16)
            for k in range(2):
                nc.gpsimd.memset(VA[k][:, :, :], 1.0)
            nc.gpsimd.memset(S[:, :, :], 0.0)
            nc.gpsimd.memset(CMB[:, :, :], 0.0)
            nc.gpsimd.memset(ZR[:, :], 0.0).then_inc(s_prep, 1)
            pool.wait_ge(s_const, 16)

            def low(m, j):
                h = HID - j * P if j == FT - 1 else P
                pool.wait_ge(s_hh, m + 1)
                need(pool, s_down, m - 1)
                nc.gpsimd.tensor_tensor(HL[j % 2][0:h, :], TH[j % 2][0:h, :], HH[j % 2][0:h, :].bitcast(F32),
                                        ALU.subtract).then_inc(s_hl, 1)

            def norm_var(norm, hb, u):
                pool.wait_ge(s_var, norm.r + 1)
                nc.gpsimd.tensor_tensor(RS[:, :], VE[:, :], CN[:, C_HALF:C_HALF + GT], ALU.pow).then_inc(s_rstd, 1)

            def norm_scale(norm, hb, u):
                if norm.kind == "A":
                    pool.wait_ge(s_xn, norm.r + 1)
                    pool.wait_ge(s_bo, 16)
                    v = X[:, bass.ds(norm.g.x, GT), :]
                    nc.gpsimd.tensor_tensor(v, v, bc(BO[:, :], 1, GT), ALU.add).then_inc(s_boa, 1)

            def ffn(buf, n, j):
                h = HID - j * P if j == FT - 1 else P
                m = n * FT + j
                if j > 0:
                    low(m - 1, j - 1)
                pool.wait_ge(s_s, m + 1)
                pool.wait_ge(s_w, m + 1)
                nc.gpsimd.tensor_tensor(TH[j % 2][0:h, :], TH[j % 2][0:h, :], CBS[ring(buf, j)][0:h, :],
                                        ALU.mult).then_inc(s_h, 1)

            def proj(g, c, hb, u):
                pool.wait_ge(s_rt, g.at * GT + c + 1)
                nc.gpsimd.tensor_tensor(RC[:, :], RC[:, :], RT[:, :], ALU.add).then_inc(s_ro, 1)

            def tail_a(n):
                low(n * FT + FT - 1, FT - 1)

            pool.sem_inc(s_ro, 1)
            run(pool, {"norm_var": norm_var, "norm_scale": norm_scale, "ffn": ffn, "proj": proj, "tail_a": tail_a})

        @block.scalar
        def _(act):
            act.wait_ge(s_const, 16)

            def routers():
                act.wait_ge(s_small, 80)
                nc.scalar.activation(WR[:, :, 0:NR], R32[:, :, :], ACT.Copy).then_inc(s_hi, 1)

            def split(k):
                act.wait_ge(s_stage[k % 2], arrive[k])
                for rows, a, b, hi, lo in pieces[k][1]:
                    nc.scalar.activation(hi, shaped(STG[k % 2][0:rows, a:b], hi), ACT.Copy).then_inc(s_hi, 1)

            def copy_high(m, j):
                h = HID - j * P if j == FT - 1 else P
                act.wait_ge(s_h, m + 1)
                need(act, s_down, m - 1)
                nc.scalar.activation(HH[j % 2][0:h, :], TH[j % 2][0:h, :], ACT.Copy).then_inc(s_hh, 1)

            def ready(u, hb):
                act.wait_ge(s_tr[u % 2], hb + u // 2 + 1)

            def norm_turn(norm, hb, u):
                for k in range(KD):
                    n = u["norm_turn"] + k
                    ready(n, hb)
                    if k == 0 and norm.prev is not None:
                        if norm.kind == "A":
                            need(act, s_qk, norm.prev * GT)
                        else:
                            act.wait_ge(s_u, norm.prev * FT + FT)
                    nc.scalar.activation(XT[norm.buf][0][:, k, :], T[n % 2][:, :], ACT.Copy).then_inc(s_xh, 1)

            def norm_first(norm, hb, u):
                if norm.kind == "A":
                    n = u["norm_first"]
                    ready(n, hb)
                    nc.scalar.activation(BT[:, :], T[n % 2][0:HEADS, :], ACT.Tanh, bias=HBG[:, 0:1],
                                         scale=0.5).then_inc(s_tf[n % 2], 1)
                else:
                    act.wait_ge(s_gap, norm.f + 1)
                    nc.scalar.activation(E2[:, :], GAP[:, :], ACT.Exp)
                    nc.scalar.activation(SGT[:, :], LG[:, :, E], ACT.Tanh, scale=0.5).then_inc(s_e2, 1)

            def norm_last(norm, hb, u):
                n = u["norm_last"]
                ready(n, hb)
                if norm.kind == "A":
                    nc.scalar.activation(DEC[:, :, 0:HEADS], T[n % 2][:, 0:GT * HEADS].rearrange("p (c h) -> p c h", c=GT),
                                         ACT.Copy).then_inc(s_dec, 1)
                else:
                    need(act, s_spread, 16 * norm.f)
                    nc.scalar.activation(CT[:, :], T[n % 2][0:NR, :], ACT.Copy).then_inc(s_tf[n % 2], 1)
                    act.wait_ge(s_tf[n % 2], hb + n // 2 + 1)
                    act.dma_start(comb_d[norm.buf, :, :], CT[:, :]).then_inc(s_spread, 16)

            def ffn(buf, n, j):
                h = HID - j * P if j == FT - 1 else P
                m = n * FT + j
                act.wait_ge(s_g, m + 1)
                need(act, s_hl, m - 1)
                nc.scalar.activation(TH[j % 2][0:h, :], PG[j % 2][0:h, :], ACT.Tanh, scale=0.5).then_inc(s_th, 1)
                if j > 0:
                    copy_high(m - 1, j - 1)
                    if j + 2 < FT:
                        load_comb(buf, n, j + 2)

            def load_comb(buf, n, j):
                k = ring(buf, j)
                for a, b, e in load_parts(j):
                    act.dma_start(CBS[k][a:b, :], comb_d[buf, e:e + 1, :].broadcast_to([b - a, GN])).then_inc(s_cl[k], 16)

            def spread(buf, n):
                act.wait_ge(s_spread, 16 * n + 16)
                need(act, s_h, n * FT - 1)
                for j in range(3):
                    load_comb(buf, n, j)

            def proj(g, c, hb, u):
                q = g.at * GT + c
                n = u["proj"] + 1
                ready(n, hb)
                act.wait_ge(s_av, q * 4 + 4)
                nc.scalar.activation(VA[c % 2][:, :, 0:DH], T[n % 2][:, 0:D].rearrange("p (h d) -> p h d", h=HEADS),
                                     ACT.Copy).then_inc(s_tf[n % 2], 1)

            def phi(g, c, hb, u):
                act.wait_ge(s_mn, g.at * GT + c + 1)
                nc.scalar.activation(RT[:, :], RT[:, :], ACT.Exp).then_inc(s_ex, 1)

            def turn(g, c, hb, u):
                n = u["turn"]
                if isinstance(g.at, int) and g.at == 0 and c == 0:
                    act.wait_ge(s_tables, 16)
                ready(n, hb)
                act.wait_ge(s_av, (g.at * GT + c) * 4 + 8)
                t = T[n % 2][:, :].rearrange("p (a b t) -> p a b t", a=2, b=2)
                nc.scalar.activation(QT[:, :, :], t[:, 0], ACT.Copy)
                nc.scalar.activation(KT[0][:, :, :], t[:, 1], ACT.Copy)
                for odd in range(2):
                    last = nc.scalar.activation(QM[0][:, :, odd, :], t[:, 0], ACT.Copy, scale=CN[:, C_PAR + odd:C_PAR + odd + 1])
                last.then_inc(s_qh, 1)

            def wo_turn(g, c, hb, u):
                n = u["wo_turn"]
                ready(n, hb)
                nc.scalar.activation(YT[0][:, :, :], T[n % 2][:, 0:D].rearrange("p (k t) -> p k t", k=KD),
                                     ACT.Copy).then_inc(s_yhi, 1)

            def tail_a(n):
                copy_high(n * FT + FT - 1, FT - 1)

            run(act, {"routers": routers, "split": split, "norm_turn": norm_turn, "norm_first": norm_first, "norm_last": norm_last,
                      "spread": spread, "ffn": ffn, "proj": proj, "phi": phi, "turn": turn, "wo_turn": wo_turn, "tail_a": tail_a})

        @block.vector
        def _(dve):
            v = nc.vector
            v.memset(R32[:, :, :], 0.0).then_inc(s_prep, 1)

            def settle():
                dve.drain()

            def split(k):
                done = split_by(k - 1)
                for rows, a, b, hi, lo in pieces[k][1]:
                    done += 1
                    dve.wait_ge(s_hi, done + 1)
                    v.tensor_tensor(lo, shaped(STG[k % 2][0:rows, a:b], hi), hi.bitcast(F32), ALU.subtract).then_inc(s_lo, 1)

            def routers():
                dve.wait_ge(s_small, 80)
                v.tensor_scalar(HBG[:, :], HBG[:, :], 0.5, None, ALU.mult)
                dve.wait_ge(s_hi, 1)
                v.tensor_tensor(WR[:, :, NR:2 * NR], R32[:, :, :], WR[:, :, 0:NR].bitcast(F32), ALU.subtract).then_inc(s_wready, 1)

            def ready(u, hb):
                dve.wait_ge(s_tr[u % 2], hb + u // 2 + 1)

            def norm_stats(norm, hb, u):
                g = norm.g
                settle()
                if norm.kind == "F1":
                    if isinstance(g.at, int) and g.at == 0:
                        dve.wait_ge(s_x0, 16)
                    elif isinstance(g.at, int) and g.at == 1:
                        dve.wait_ge(s_x1, 16)
                    else:
                        dve.wait_ge(s_xrest, 16 * g.at - 16)
                for c in range(GT):
                    v.bn_stats(ST[:, c, :], X[:, g.x + c, :])

            def norm_var(norm, hb, u):
                settle()
                for c in range(GT):
                    v.bn_aggr(MV[:, c, :], ST[:, c, :])
                settle()
                v.tensor_scalar(VE[:, :], MV[:, :, 1], LN_EPS, None, ALU.add).then_inc(s_var, 1)

            def norm_scale(norm, hb, u):
                dve.wait_ge(s_rstd, norm.r + 1)
                for c in range(GT):
                    last = v.tensor_scalar(XN[:, c, :], X[:, norm.g.x + c, :], MV[:, c, 0:1], RS[:, c:c + 1],
                                           ALU.subtract, ALU.mult)
                last.then_inc(s_xn, 1)

            def norm_turn(norm, hb, u):
                for k in range(KD):
                    n = u["norm_turn"] + k
                    dve.wait_ge(s_xh, norm.r * KD + k + 1)
                    v.tensor_tensor(XT[norm.buf][1][:, k, :], T[n % 2][:, :], XT[norm.buf][0][:, k, :].bitcast(F32),
                                    ALU.subtract).then_inc(s_tf[n % 2], 1)

            def norm_first(norm, hb, u):
                n = u["norm_first"]
                if norm.kind == "A":
                    dve.wait_ge(s_tf[n % 2], hb + n // 2 + 1)
                    v.tensor_scalar(BT[:, :], BT[:, :], 0.5, 0.5, ALU.mult, ALU.add)
                    settle()
                    v.tensor_scalar(BT[:, :], BT[:, :], BETA_MIN, BETA_MAX, ALU.max, ALU.min)
                    settle()
                    for c in range(GT):
                        t = slice(c * P, (c + 1) * P)
                        last = v.tensor_tensor_scan(DP[:, t], BT[:, t], ZR[:, :], 1.0, ALU.mult, ALU.add)
                    last.then_inc(s_dp, 1)
                    return
                if isinstance(norm.r, int) and norm.r == 0:
                    dve.wait_ge(s_const, 16)
                ready(n, hb)
                t = T[n % 2][:, 0:GT * 2 * NR].rearrange("p (c a e) -> p c a e", c=GT, a=2)
                v.tensor_copy(LG[:, :, :], t[:, :, 1, :])
                settle()
                v.tensor_tensor(LG[:, :, :], t[:, :, 0, :], LG[:, :, :], ALU.add).then_inc(s_tf[n % 2], 1)
                settle()
                for c in range(GT):
                    v.max(TOP[:, c, :], LG[:, c, 0:E])
                settle()
                v.tensor_tensor(GAP[:, :], TOP[:, :, 1], TOP[:, :, 0], ALU.subtract).then_inc(s_gap, 1)
                for c in range(GT):
                    v.max_index(IDX[:, c, :], TOP[:, c, :], LG[:, c, 0:E])
                settle()
                v.tensor_copy(IDF[:, :, :], IDX[:, :, 0:2])
                settle()
                for k in range(2):
                    v.tensor_tensor(HOT[:, k], bc(CN[:, C_IOTA:C_IOTA + E], 1, GT), bc(IDF[:, :, k], 2, E), ALU.is_equal)

            def norm_mid(norm, hb, u):
                if norm.kind == "A":
                    return
                dve.wait_ge(s_e2, norm.f + 1)
                v.tensor_scalar(DEN2[:, :], E2[:, :], 4.0, 4.0, ALU.mult, ALU.add)
                v.tensor_scalar(CMB[:, :, E], SGT[:, :], 1.0, 0.125, ALU.add, ALU.mult)
                settle()
                v.reciprocal(W12[:, 0, :], DEN2[:, :])
                settle()
                v.tensor_tensor(W12[:, 1, :], W12[:, 0, :], E2[:, :], ALU.mult)
                settle()
                v.tensor_tensor(HOT[:, :, :, :], HOT[:, :, :, :], bc(W12[:, :, :], 3, E), ALU.mult)
                settle()
                v.tensor_tensor(CMB[:, :, 0:E], HOT[:, 0], HOT[:, 1], ALU.add).then_inc(s_comb, 1)

            def norm_last(norm, hb, u):
                if norm.kind == "A":
                    n = u["norm_last"]
                    if isinstance(norm.r, int) and norm.r == 2:
                        dve.wait_ge(s_tables, 16)
                    dve.wait_ge(s_dec, norm.g.at + 1)
                    ready(n, hb)
                    v.tensor_tensor(PT[:, :, :], T[n % 2][:, P:P + 2 * GT].rearrange("p (a c) -> p a c", a=2),
                                    bc(CN[:, bass.ds(norm.g.at * GT + C_KEEP, GT)], 1, 2), ALU.mult).then_inc(s_tf[n % 2], 1)
                    v.reciprocal(DEC[:, :, HEADS:2 * HEADS], DEC[:, :, 0:HEADS])

            def ffn(buf, n, j):
                h = HID - j * P if j == FT - 1 else P
                m = n * FT + j
                dve.wait_ge(s_th, m + 1)
                v.scalar_tensor_tensor(TH[j % 2][0:h, :], TH[j % 2][0:h, :], 1.0, PG[j % 2][0:h, :], ALU.add, ALU.mult).then_inc(s_s, 1)
                k = ring(buf, j)
                dve.wait_ge(s_cl[k], ring_loads(n, buf, j))
                dve.wait_ge(s_u, m + 1)
                v.tensor_tensor(CBS[k][0:h, :], PU[0:h, :], CBS[k][0:h, :], ALU.mult).then_inc(s_w, 1)

            def tail_b(n, g, final):
                dve.wait_ge(s_down, n * FT + FT)
                for b in range(2):
                    xv = X[:, bass.ds(g.x + 2 * b, 2), :]
                    last = v.tensor_tensor(xv, PY[b][:, :].rearrange("p (t d) -> p t d", t=2), xv, ALU.add)
                    if b == 1:
                        last.then_inc(s_yr, 1)
                if final:
                    settle()
                    v.sem_inc(s_out, 1)

            def proj(g, c, hb, us):
                q = g.at * GT + c
                u = us["proj"]
                ready(u, hb)
                dve.wait_ge(s_ro, q + 1)
                t = T[u % 2][:, :].rearrange("p (h a d) -> p h a d", a=2, d=8)
                tb = rope[:, g.at * GT + c, :]
                rc = RC[:, :].rearrange("p (h a d) -> p h a d", a=2, d=8)
                rt = RT[:, :].rearrange("p (h a d) -> p h a d", a=2, d=8)
                cos = bc(bc(tb[:, 0:8], 1, 2), 1, 2 * HEADS)
                v.tensor_tensor(rc, t, cos, ALU.mult)
                sin = bc(tb[:, 8:16], 1, 2 * HEADS)
                v.scalar_tensor_tensor(rt[:, :, 0, :], t[:, :, 1, :], -1.0, sin, ALU.mult, ALU.mult)
                v.tensor_tensor(rt[:, :, 1, :], t[:, :, 0, :], sin, ALU.mult).then_inc(s_rt, 1)
                dve.wait_ge(s_rt, q + 1)
                v.sem_inc(s_tf[u % 2], 1)

            def phi(g, c, hb, us):
                q = g.at * GT + c
                dve.wait_ge(s_ro, q + 2)
                v.tensor_scalar(RT[:, :], RC[:, :], 0.0, None, ALU.min).then_inc(s_mn, 1)
                dve.wait_ge(s_ex, q + 1)
                v.scalar_tensor_tensor(RC[:, :], RC[:, :], 0.0, RT[:, :], ALU.max, ALU.add)
                settle()
                if c == 0:
                    dve.wait_ge(s_dec, g.at + 1)
                dve.wait_ge(s_av, q * 4 + 4)
                v.tensor_tensor(QK[c % 2][:, :].rearrange("p (h d) -> p h d", d=DH),
                                RC[:, :].rearrange("p (h d) -> p h d", d=DH),
                                bc(DEC[:, c, :], 2, DH), ALU.mult).then_inc(s_qk, 1)

            def turn(g, c, hb, us):
                n = us["turn"]
                dve.wait_ge(s_qh, g.at * GT + c + 1)
                t = T[n % 2][:, :].rearrange("p (a b t) -> p a b t", a=2, b=2)
                for odd in range(2):
                    v.scalar_tensor_tensor(QM[1][:, :, odd, :], t[:, 0], CN[:, C_PAR + odd:C_PAR + odd + 1],
                                           QM[0][:, :, odd, :].bitcast(F32), ALU.mult, ALU.subtract)
                v.tensor_tensor(KT[1][:, :, :], t[:, 1], KT[0][:, :, :].bitcast(F32), ALU.subtract).then_inc(s_tf[n % 2], 1)

            def masked(q, b, n, hb):
                ready(n, hb)
                dve.wait_ge(s_av, q * 4 + b + 7)
                v.tensor_tensor(AM[b % 2], T[n % 2][:, :].rearrange("p (h t) -> p h t", h=4),
                                bc(CN[:, C_CAUSAL:C_CAUSAL + P], 1, 4), ALU.mult).then_inc(s_tf[n % 2], 1)

            def core(g, c, hb, us):
                q = g.at * GT + c
                n = us["core"]
                ready(n, hb)
                v.tensor_tensor(DS[:, :, :], T[n % 2][:, 0:16 * VW].rearrange("p (a n) -> p a n", a=2), block2,
                                ALU.mult).then_inc(s_tf[n % 2], 1)
                masked(q, 0, n + 1, hb)

            def core_1(g, c, hb, us):
                masked(g.at * GT + c, 1, us["core_1"], hb)
                v.tensor_tensor(DS[:, :, :], S[:, :, :], DS[:, :, :], ALU.add)

            def core_2(g, c, hb, us):
                q = g.at * GT + c
                masked(q, 2, us["core_2"], hb)
                settle()
                dve.wait_ge(s_inter, q + 1)
                for a in range(2):
                    last = v.tensor_scalar(S[:, a, :], DS[:, a, :], PT[:, a, c:c + 1], None, ALU.mult)
                last.then_inc(s_st, 1)

            def core_3(g, c, hb, us):
                masked(g.at * GT + c, 3, us["core_3"], hb)

            def attend(g, c, hb, us):
                q = g.at * GT + c
                dve.wait_ge(s_av, q * 4 + 12)
                o = T2[:, 0:HEADS * VW].rearrange("p (h d) -> p h d", d=VW)
                v.tensor_scalar(DN[:, :], o[:, :, DH], DEN_EPS, None, ALU.add)
                settle()
                v.reciprocal(RD[:, :], DN[:, :])
                settle()
                v.tensor_tensor(Y[:, :, :], o[:, :, 0:DH], bc(RD[:, :], 2, DH), ALU.mult).then_inc(s_or, 1)

            def wo_turn(g, c, hb, us):
                q = g.at * GT + c
                n = us["wo_turn"]
                dve.wait_ge(s_yhi, q + 1)
                v.tensor_tensor(YT[1][:, :, :], T[n % 2][:, 0:D].rearrange("p (k t) -> p k t", k=KD),
                                YT[0][:, :, :].bitcast(F32), ALU.subtract).then_inc(s_tf[n % 2], 1)

            def wo(g, c, hb, us):
                n = us["wo"]
                dve.wait_ge(s_boa, g.at + 1)
                ready(n, hb)
                xv = X[:, g.x + c, :]
                v.tensor_tensor(xv, T[n % 2][:, 0:D], xv, ALU.add).then_inc(s_tf[n % 2], 1)

            v.sem_inc(s_st, 1)
            v.sem_inc(s_or, 1)
            run(dve, {"routers": routers, "split": split, "norm_stats": norm_stats, "norm_var": norm_var, "norm_scale": norm_scale,
                      "norm_turn": norm_turn, "norm_first": norm_first, "norm_mid": norm_mid, "norm_last": norm_last, "ffn": ffn, "tail_b": tail_b,
                      "proj": proj, "phi": phi, "turn": turn, "core": core, "core_1": core_1, "core_2": core_2, "core_3": core_3,
                      "attend": attend, "wo_turn": wo_turn, "wo": wo})

        @block.tensor
        def _(pe):
            mm = nc.tensor.matmul
            PASSES = ((0, 0), (0, 1), (1, 0))

            def fresh(u, hb):
                need(pe, s_tf[u % 2], hb + u // 2)

            def taken(u, hb):
                pe.wait_ge(s_tf[u % 2], hb + u // 2 + 1)

            def routers():
                pe.wait_ge(s_wready, 1)

            def norm_turn(norm, hb, us):
                pe.wait_ge(s_xn, norm.r + 1)
                for k in range(KD):
                    u = us["norm_turn"] + k
                    fresh(u, hb)
                    for c in range(GT):
                        last = nc.tensor.transpose(T[u % 2][:, c * P:(c + 1) * P], XN[:, c, k * P:(k + 1) * P], ident)
                    last.then_inc(s_tr[u % 2], 1)

            def norm_first(norm, hb, us):
                kind = norm.kind
                u = us["norm_first"]
                taken(us["norm_turn"] + (us["norm_turn"] + u + 1) % 2, hb)
                fresh(u, hb)
                if kind == "A":
                    n = 0
                    for k in range(KD):
                        for a, b in PASSES:
                            last = mm(T[u % 2][0:HEADS, :], WP[b][:, k, 3 * D:QKV], XT[norm.buf][a][:, k, :],
                                      start=n == 0, stop=n == 3 * KD - 1)
                            n += 1
                else:
                    for c in range(GT):
                        at = c * 2 * NR
                        for k in range(KD):
                            for a in range(2):
                                w = (2 - a) * NR
                                last = mm(T[u % 2][:, at:at + w], XT[norm.buf][a][:, k, c * P:(c + 1) * P], WR[:, k, 0:w],
                                          start=k == 0 and a == 0, stop=k == KD - 1 and a == 1, skip_group_check=True)
                last.then_inc(s_tr[u % 2], 1)

            def norm_last(norm, hb, us):
                u = us["norm_last"]
                fresh(u, hb)
                if norm.kind == "A":
                    if isinstance(norm.r, int) and norm.r == 2:
                        pe.wait_ge(s_tables, 16)
                    pe.wait_ge(s_dp, norm.g.at + 1)
                    ends = DP[:, :].rearrange("h (c t) -> h c t", c=GT)[:, :, P - 1]
                    for a in range(2):
                        mm(T[u % 2][:, P + a * GT:P + (a + 1) * GT], expand[:, a, :], ends, start=True, stop=True)
                    for c in range(GT):
                        last = nc.tensor.transpose(T[u % 2][:, c * HEADS:(c + 1) * HEADS], DP[:, c * P:(c + 1) * P],
                                                   CN[0:HEADS, C_ID:C_ID + HEADS])
                else:
                    pe.wait_ge(s_comb, norm.f + 1)
                    for c in range(GT):
                        last = nc.tensor.transpose(T[u % 2][0:NR, c * P:(c + 1) * P], CMB[:, c, :], ident)
                last.then_inc(s_tr[u % 2], 1)

            def down(n, j):
                h = HID - j * P if j == FT - 1 else P
                m = n * FT + j
                pe.wait_ge(s_hl, m + 1)
                if isinstance(n, int) and n == 0 and j in PART_AT:
                    pe.wait_ge(s_lo, split_by(3 * PART_AT.index(j) + 2))
                if j == 0:
                    need(pe, s_yr, n)
                for t in range(GT):
                    for i, (a, b) in enumerate(PASSES):
                        last = mm(PY[t // 2][:, (t % 2) * D:(t % 2 + 1) * D], (HH, HL)[a][j % 2][0:h, t * P:(t + 1) * P],
                                  WD[b][0:h, j, :], start=(j == 0 and i == 0 and t % 2 == 0),
                                  stop=(j == FT - 1 and i == 2), skip_group_check=True)
                last.then_inc(s_down, 1)

            def ffn(buf, n, j):
                h = HID - j * P if j == FT - 1 else P
                m = n * FT + j
                col = slice(j * P, j * P + h)
                if isinstance(n, int) and n == 0 and j in PART_AT:
                    pe.wait_ge(s_lo, split_by(3 * PART_AT.index(j) + 1))
                for w, out, free, before, ready in ((WG, PG[j % 2], s_s, 1, s_g), (WU, PU, s_w, 0, s_u)):
                    need(pe, free, m - before)
                    i = 0
                    for k in range(KD):
                        for a, b in PASSES:
                            last = mm(out[0:h, :], w[b][:, k, col], XT[buf][a][:, k, :], start=i == 0, stop=i == 3 * KD - 1)
                            i += 1
                    last.then_inc(ready, 1)

            def proj(g, c, hb, us):
                for u, n0, n1 in ((us["proj"], 0, 2 * D), (us["proj"] + 1, 2 * D, 3 * D)):
                    fresh(u, hb)
                    i = 0
                    for k in range(KD):
                        for a, b in PASSES:
                            last = mm(T[u % 2][:, 0:n1 - n0], XT["A"][a][:, k, c * P:(c + 1) * P], WP[b][:, k, n0:n1],
                                      start=i == 0, stop=i == 3 * KD - 1)
                            i += 1
                    last.then_inc(s_tr[u % 2], 1)

            def turn(g, c, hb, us):
                u = us["turn"]
                pe.wait_ge(s_qk, g.at * GT + c + 1)
                fresh(u, hb)
                for b in range(4):
                    last = nc.tensor.transpose(T[u % 2][:, b * P:(b + 1) * P], QK[c % 2][:, b * P:(b + 1) * P], ident)
                last.then_inc(s_tr[u % 2], 1)

            def scores(b, u, hb):
                fresh(u, hb)
                row = 32 * b
                for a in range(2):
                    for n, (k, q) in enumerate(PASSES):
                        last = mm(T[u % 2][:, a * 2 * P:(a + 1) * 2 * P], KT[k][row:row + 32, a, :],
                                  QM[q][row:row + 32, a, :, :], start=n == 0, stop=n == 2)
                last.then_inc(s_tr[u % 2], 1)

            def values(c, b, u, hb):
                taken(u, hb)
                for i in range(4):
                    hd = 8 * (i // 2) + 2 * b + i % 2
                    last = mm(T2[:, hd * VW:(hd + 1) * VW], AM[b % 2][:, i, :], VA[c % 2][:, hd, :], start=False,
                              stop=hd == HEADS - 1, skip_group_check=True)
                last.then_inc(s_av, 1)

            def core(g, c, hb, us):
                q = g.at * GT + c
                pe.wait_ge(s_qh, q + 1)
                pe.wait_ge(s_st, q + 1)
                pe.wait_ge(s_or, q + 1)
                for a in range(2):
                    last = mm(T2[:, a * 8 * VW:(a + 1) * 8 * VW], QT[:, a, :], S[:, a, :], start=a == 0, stop=False,
                              skip_group_check=True)
                last.then_inc(s_inter, 1)
                u = us["core"]
                fresh(u, hb)
                for a in range(2):
                    last = mm(T[u % 2][:, a * 8 * VW:(a + 1) * 8 * VW], QK[c % 2][:, D + a * P:D + (a + 1) * P],
                              VA[c % 2][:, 8 * a:8 * a + 8, :], start=True, stop=True)
                last.then_inc(s_tr[u % 2], 1)
                if (us["turn"] - u - 1) % 2:
                    taken(us["turn"], hb)
                scores(0, u + 1, hb)

            def core_1(g, c, hb, us):
                values(c, 0, us["core"] + 1, hb)
                scores(1, us["core_1"], hb)

            def core_2(g, c, hb, us):
                values(c, 1, us["core_1"], hb)
                scores(2, us["core_2"], hb)

            def core_3(g, c, hb, us):
                values(c, 2, us["core_2"], hb)
                scores(3, us["core_3"], hb)

            def core_4(g, c, hb, us):
                values(c, 3, us["core_3"], hb)

            def wo_turn(g, c, hb, us):
                u = us["wo_turn"]
                pe.wait_ge(s_or, g.at * GT + c + 2)
                fresh(u, hb)
                yv = Y[:, :, :].rearrange("p h d -> p (h d)")
                for k in range(KD):
                    last = nc.tensor.transpose(T[u % 2][:, k * P:(k + 1) * P], yv[:, k * P:(k + 1) * P], ident)
                last.then_inc(s_tr[u % 2], 1)

            def wo(g, c, hb, us):
                u = us["wo"]
                if (us["wo_turn"] - u) % 2:
                    taken(us["wo_turn"], hb)
                fresh(u, hb)
                i = 0
                for k in range(KD):
                    for a, b in PASSES:
                        last = mm(T[u % 2][:, 0:D], YT[a][:, k, :], WO[b][:, k, :], start=i == 0, stop=i == 3 * KD - 1)
                        i += 1
                last.then_inc(s_tr[u % 2], 1)

            def tail_a(n):
                down(n, FT - 2)

            def tail_b(n, g, final):
                down(n, FT - 1)

            pe.sem_inc(s_av, 8)
            pe.wait_ge(s_const, 16)
            run(pe, {"routers": routers, "norm_turn": norm_turn, "norm_first": norm_first, "norm_last": norm_last, "ffn": ffn, "tail_a": tail_a,
                     "tail_b": tail_b, "down": down, "proj": proj, "turn": turn, "core": core, "core_1": core_1, "core_2": core_2,
                     "core_3": core_3, "core_4": core_4, "wo_turn": wo_turn, "wo": wo})


_INS = ["L0_attn_x", "L0_attn_Wq", "L0_attn_Wk", "L0_attn_Wv", "L0_attn_Wg", "L0_attn_bg", "L0_attn_Wo", "L0_attn_bo",
        "L0_ffn_gate_w", "L0_ffn_w_gate", "L0_ffn_w_up", "L0_ffn_w_down", "L0_ffn_shgate_w", "L0_ffn_shw_gate",
        "L0_ffn_shw_up", "L0_ffn_shw_down"]


def kernel(**inputs):
    import concourse.bacc as _bacc
    from concourse.bass_utils import run_bass_kernel_spmd as _run

    nc = _bacc.Bacc("TRN2", target_bir_lowering=False, num_devices=1)
    arrays, args = {}, []
    for name in _INS:
        a = np.ascontiguousarray(inputs[name])
        arrays[f"in_{name}"] = a
        args.append(nc.dram_tensor(f"in_{name}", a.shape, mybir.dt.from_np(a.dtype), kind="ExternalInput").ap())
    c = constants()
    arrays["in_constants"] = c
    args.append(nc.dram_tensor("in_constants", c.shape, F32, kind="ExternalInput").ap())
    args.append(nc.dram_tensor("combine", (2, NR, GN), F32).ap())
    args.append(nc.dram_tensor("out", (B, L, D), F32, kind="ExternalOutput").ap())
    build(nc, *args)
    r = _run(nc, [arrays], core_ids=[0])
    return r.results[0]["out"]
```
